# Optimizing a Trainium2 kernel written in Bass

```python
import numpy as np
import jax
import jax.numpy as jnp

def _softmax(x, axis=-1):
    return jax.nn.softmax(x, axis=axis)

def _gelu(x):
    return jax.nn.gelu(x, approximate=True)

def _silu(x):
    return jax.nn.silu(x)

def _sigmoid(x):
    return jax.nn.sigmoid(x)

def _layernorm(x, axis=-1, eps=1e-05):
    m = jnp.mean(x, axis=axis, keepdims=True)
    v = jnp.var(x, axis=axis, keepdims=True)
    return (x - m) / jnp.sqrt(v + eps)

def _scatter_add(tgt, idx, src, axis=0):
    return tgt.at[idx].add(src)

def _segment_sum(src, seg, n):
    return jax.ops.segment_sum(src, seg, n)
kernel_name = 'mk_adaln_ffn_d1_seqx_r4_4a0a41'

def setup_inputs(seed: int=0):
    np.random.seed(seed)
    _w = jnp.asarray

    def _rec_inputs():
        import jax
        import jax.numpy as jnp
        _rk = jax.random.key(seed)
        x = -7.109e-05 + 0.9999 * jax.random.normal(jax.random.fold_in(_rk, 1), (2, 1024, 256), jnp.float32)
        _lenS = 1024 - jax.random.randint(jax.random.fold_in(_rk, 7), (2,), 0, max(1, 1024 // 4) + 1, jnp.int32)
        _lenS2 = 1024 - jax.random.randint(jax.random.fold_in(_rk, 8), (2,), 0, max(1, 1024 // 4) + 1, jnp.int32)
        cond_1024 = 0.00191187 + 0.999416 * jax.random.normal(jax.random.fold_in(_rk, 11), (2, 256), jnp.float32)
        return (x, cond_1024)
    x, cond_1024 = _rec_inputs()

    def _L0_cond_setup():
        import jax, jax.numpy as jnp
        import numpy as np
        N, T, D, H = (64, 64, 256, 256)
        key = jax.random.key(seed)
        k1, k2, k3, k4 = jax.random.split(key, 4)
        x = jax.random.normal(k1, (N, T, D), dtype=jnp.float32)
        h0 = jax.random.normal(k2, (N, H), dtype=jnp.float32)
        Wx = jax.random.normal(k3, (D, H), dtype=jnp.float32) / jnp.sqrt(jnp.float32(D))
        Wh = jax.random.normal(k4, (H, H), dtype=jnp.float32) / jnp.sqrt(jnp.float32(H))
        b = jnp.zeros((H,), dtype=jnp.float32)
        return {'x': x, 'h0': h0, 'Wx': Wx, 'Wh': Wh, 'b': b}
    _L0_cond_all = _L0_cond_setup()
    _L0_cond_in = {k: v for k, v in _L0_cond_all.items() if k in ('Wx', 'Wh', 'b')}
    del _L0_cond_all

    def _L0_ffn_setup():
        import jax, jax.numpy as jnp
        import numpy as np
        B, S, H = (2, 512, 256)
        E, I, K = (8, 1024, 2)

        def _moe_forward(x, gate_w, wg, wu, wd):
            b, s, h = x.shape
            x_flat = x.reshape(-1, h)
            logits = x_flat @ gate_w.T
            top_v, top_i = jax.lax.top_k(logits, K)
            probs = jax.nn.softmax(top_v.astype(jnp.float32), axis=-1).astype(logits.dtype)
            one_hot = jax.nn.one_hot(top_i, E, dtype=probs.dtype)
            combine = jnp.einsum('tk,tke->et', probs, one_hot)

            def body(acc, ws):
                wge, wue, wde, we = ws
                hidden = jax.nn.silu(x_flat @ wge.T) * (x_flat @ wue.T)
                return (acc + we[:, None] * (hidden @ wde.T), None)
            out, _ = jax.lax.scan(body, jnp.zeros_like(x_flat), (wg, wu, wd, combine))
            return out.reshape(b, s, h)
        key = jax.random.key(seed)
        ks = jax.random.split(key, 5)
        scale_h = 1.0 / np.sqrt(H)
        scale_i = 1.0 / np.sqrt(I)
        x = jax.random.normal(ks[0], (B, S, H), dtype=jnp.float32)
        gate_w = jax.random.normal(ks[1], (E, H), dtype=jnp.float32) * scale_h
        wg = jax.random.normal(ks[2], (E, I, H), dtype=jnp.float32) * scale_h
        wu = jax.random.normal(ks[3], (E, I, H), dtype=jnp.float32) * scale_h
        wd = jax.random.normal(ks[4], (E, H, I), dtype=jnp.float32) * scale_i
        return {'x': x, 'gate_w': gate_w, 'wg': wg, 'wu': wu, 'wd': wd}
    _L0_ffn_all = _L0_ffn_setup()
    _L0_ffn_in = {k: v for k, v in _L0_ffn_all.items() if k in ('gate_w', 'wg', 'wu', 'wd')}
    del _L0_ffn_all
    return {'x': x, 'cond_1024': cond_1024, 'L0_cond_Wx': _L0_cond_in['Wx'], 'L0_cond_Wh': _L0_cond_in['Wh'], 'L0_cond_b': _L0_cond_in['b'], 'L0_ffn_gate_w': _L0_ffn_in['gate_w'], 'L0_ffn_wg': _L0_ffn_in['wg'], 'L0_ffn_wu': _L0_ffn_in['wu'], 'L0_ffn_wd': _L0_ffn_in['wd']}

def reference(x, cond_1024, L0_cond_Wx, L0_cond_Wh, L0_cond_b, L0_ffn_gate_w, L0_ffn_wg, L0_ffn_wu, L0_ffn_wd):
    import jax
    import jax.numpy as jnp

    def _L0_cond_ref(x, h0, Wx, Wh, b):
        import jax, jax.numpy as jnp
        import numpy as np
        N, T, D, H = (64, 64, 256, 256)
        xW = jnp.einsum('ntd,dh->nth', x, Wx) + b

        def step(prev_h, xw_t):
            next_h = jnp.tanh(xw_t + prev_h @ Wh)
            return (next_h, next_h)
        _, hs = jax.lax.scan(step, h0, jnp.swapaxes(xW, 0, 1))
        return jnp.swapaxes(hs, 0, 1)

    def _L0_ffn_ref(x, gate_w, wg, wu, wd):
        import jax, jax.numpy as jnp
        import numpy as np
        B, S, H = (2, 512, 256)
        E, I, K = (8, 1024, 2)

        def _moe_forward(x, gate_w, wg, wu, wd):
            b, s, h = x.shape
            x_flat = x.reshape(-1, h)
            logits = x_flat @ gate_w.T
            top_v, top_i = jax.lax.top_k(logits, K)
            probs = jax.nn.softmax(top_v.astype(jnp.float32), axis=-1).astype(logits.dtype)
            one_hot = jax.nn.one_hot(top_i, E, dtype=probs.dtype)
            combine = jnp.einsum('tk,tke->et', probs, one_hot)

            def body(acc, ws):
                wge, wue, wde, we = ws
                hidden = jax.nn.silu(x_flat @ wge.T) * (x_flat @ wue.T)
                return (acc + we[:, None] * (hidden @ wde.T), None)
            out, _ = jax.lax.scan(body, jnp.zeros_like(x_flat), (wg, wu, wd, combine))
            return out.reshape(b, s, h)
        return _moe_forward(x, gate_w, wg, wu, wd)
    x = x + _L0_ffn_ref(_L0_cond_ref(x, cond_1024, L0_cond_Wx, L0_cond_Wh, L0_cond_b), L0_ffn_gate_w, L0_ffn_wg, L0_ffn_wu, L0_ffn_wd)
    return x

_drawn_inputs = setup_inputs


def setup_inputs(seed=0):
    import zlib

    import numpy as np

    out = dict(_drawn_inputs(seed))
    spreads = {'L0_cond_b': (0.0, 0.1)}
    factors = {}
    for name, (base, spread) in spreads.items():
        noise = np.random.default_rng([zlib.crc32(name.encode()), seed]).standard_normal(out[name].shape)
        drawn = base * np.exp(spread * noise) if base else spread * noise
        out[name] = jnp.asarray(drawn.astype(out[name].dtype))
    for name, factor in factors.items():
        out[name] = (out[name] * factor).astype(out[name].dtype)
    return out
```

```python
from contextlib import ExitStack

import concourse.bass as bass
from concourse import mybir

F32 = mybir.dt.float32
F16 = mybir.dt.float16
I32 = mybir.dt.int32
U32 = mybir.dt.uint32
ALU = mybir.AluOpType
ACT = mybir.ActivationFunctionType
AX = mybir.AxisListType

P = 128
SCALE = 16.0
NEG = -3.0e38


def build(nc, xT, x, h0T, wx, wh, bias, gateT, w_all, out):
    B, T, D = x.shape
    H = wh.shape[0]
    E = gateT.shape[2]
    KC = H // P
    TOK = B * T
    STEPS = P // B
    NBLK = T // STEPS
    WCOL = w_all.shape[2]
    INNER = WCOL // (3 * KC)
    IC = INNER // P
    GU = KC * 2 * INNER
    XT_W = STEPS * B
    PAIRS = NBLK // 2
    CHUNK = 384
    NCH = E * WCOL // CHUNK
    CH_PAIR = NCH // PAIRS
    REGION = TOK + P
    ROW = 2 * H
    MAXT = 2 * TOK // P + E - 1
    MINT = 2 * TOK // P
    assert KC == 2 and INNER == 1024 and NCH % PAIRS == 0

    rows_dram = nc.dram_tensor("expert_rows", (E * REGION, ROW), F16, kind="Internal").ap()
    y_dram = nc.dram_tensor("expert_out", (MAXT * P, H), F32, kind="Internal").ap()
    w_cols = w_all.rearrange("p e c -> p (e c)")

    with ExitStack() as outer:
        def sb(name, shape, dt, ctx=outer):
            return ctx.enter_context(nc.sbuf_tensor(name, shape, dt))

        def sem(name, ctx=outer):
            return ctx.enter_context(nc.semaphore(name))

        ident32 = sb("ident32", [P, P], F32)
        ident16 = sb("ident16", [P, P], F16)
        stats = sb("stats", [P, NBLK, 4], F32)
        table = sb("table", [1, 2, MAXT + 1], I32)
        ntiles = sb("ntiles", [1, 1], I32)
        probs = sb("probs", [P, 2, NBLK], F32)
        places = sb("places", [P, 2, NBLK], I32)

        with ExitStack() as wctx:
            w_hi = sb("w_hi", [P, E, WCOL], F16, wctx)
            w_lo = sb("w_lo", [P, E, WCOL], F16, wctx)
            recurrence(nc, locals())
            experts(nc, locals())
        combine(nc, locals())


def recurrence(nc, g):
    xT, h0T, wx, wh, bias, gateT, w_cols = (g[k] for k in ("xT", "h0T", "wx", "wh", "bias", "gateT", "w_cols"))
    rows_dram, w_hi, w_lo = g["rows_dram"], g["w_hi"], g["w_lo"]
    ident32, ident16, stats, table, ntiles, probs, places = (
        g[k] for k in ("ident32", "ident16", "stats", "table", "ntiles", "probs", "places"))
    H, E, B, T, STEPS, NBLK, PAIRS = (g[k] for k in ("H", "E", "B", "T", "STEPS", "NBLK", "PAIRS"))
    CHUNK, CH_PAIR, REGION, ROW, MAXT, MINT = (
        g[k] for k in ("CHUNK", "CH_PAIR", "REGION", "ROW", "MAXT", "MINT"))
    y_dram = g["y_dram"]
    WIN = 2 * STEPS
    w_hi_cols = w_hi[:].rearrange("p e c -> p (e c)")
    w_lo_cols = w_lo[:].rearrange("p e c -> p (e c)")

    with ExitStack() as ctx:
        def sb(name, shape, dt):
            return ctx.enter_context(nc.sbuf_tensor(name, shape, dt))

        def ps(name, shape, dt):
            return ctx.enter_context(nc.psum_tensor(name, shape, dt))

        def sem(name):
            return ctx.enter_context(nc.semaphore(name))

        wx_sb = sb("wx_sb", [P, 2, H], F32)
        wh_hi = sb("wh_hi", [P, 2, H], F16)
        wh_lo = sb("wh_lo", [P, 2, H], F16)
        gate_hi = sb("gate_hi", [P, 2, E], F16)
        gate_lo = sb("gate_lo", [P, 2, E], F16)
        b_sb = sb("b_sb", [1, H], F32)
        ones = sb("ones", [1, STEPS], F32)
        h0 = sb("h0", [P, 2, B], F32)
        hi = sb("hi", [P, 2, 2, P], F16)
        lo = sb("lo", [P, 2, 2, P], F16)
        xt = sb("xt", [P, 2, 2, P], F32)
        rows = sb("rows", [P, ROW], F16)
        stage = sb("stage", [P, 2, CHUNK], F32)
        flat = stage[:].rearrange("p a c -> p (a c)")
        wh_sb = flat[:, 0:2 * H].rearrange("p (k n) -> p k n", k=2)
        gate_sb = flat[:, 2 * H:2 * H + 2 * E].rearrange("p (k e) -> p k e", k=2)
        zero_rows = flat[:, 0:H].bitcast(F16)
        tri8 = flat[:, H:H + E * E].rearrange("p (a b) -> p a b", a=E)
        cnt_i = flat[:, H + E * E:H + E * E + E].bitcast(I32)
        slots = flat[:, 2 * H:2 * H + 2 * NBLK]
        moved = flat[:, 2 * H + 2 * NBLK:2 * H + 4 * NBLK]
        cells, at = {}, 0
        xflat = xt[:].rearrange("p a k c -> p (a k c)")
        for name, n in dict(cmp=(MAXT + 1) * E, cnt=E, nt=E, end=E, ej=MAXT + 1, sj=MAXT + 1, qrow=T // STEPS,
                            jrow=MAXT + 1).items():
            cells[name] = xflat[:, at:at + n]
            at += n
        cmp, cnt, nt, end, ej, sj, qrow, jrow = cells.values()
        tri = sb("tri", [P, P], F16)
        all1 = sb("all1", [P, P], F16)
        rev = sb("rev", [P, E], F32)
        base = sb("base", [P, E], F32)
        seen = sb("seen", [P, 2, E], F16)
        lg = sb("lg", [P, E], F32)
        lg2 = sb("lg2", [P, E], F32)
        pick = sb("pick", [P, E], F32)
        oh1 = sb("oh1", [P, E], F32)
        oh2 = sb("oh2", [P, E], F32)
        chosen = sb("chosen", [P, E], F16)
        rank = sb("rank", [P, E], F32)
        r1 = sb("r1", [P, 1], F32)
        st = sb("st", [P, 4], F32)
        slot = sb("slot", [P, 2], I32)

        xw = [[ps(f"xw{i}{p}", [P, 512], F32) for p in range(2)] for i in range(2)]
        h32 = ps("h32", [P, 512], F32)
        p_rows = ps("p_rows", [P, 2 * ROW], F16)
        p_lg = ps("p_lg", [P, 512], F32)
        p_rank = ps("p_rank", [P, 512], F32)

        s_w = sem("a_weights_in")
        s_x = [sem("a_x_in0"), sem("a_x_in1")]
        s_wst = [sem("a_stage_in0"), sem("a_stage_in1")]
        s_cst = sem("a_consts")
        s_prep = sem("a_prep")
        s_xw = sem("a_xw_done")
        s_pre = sem("a_preact")
        s_hi = sem("a_h_hi")
        s_h32 = sem("a_h32")
        s_lo = sem("a_h_lo")
        s_lg = sem("a_logits")
        s_tr = sem("a_rows_T")
        s_rows = sem("a_rows_sb")
        s_rt = sem("a_route")
        s_rk = sem("a_rank")
        s_sc = sem("a_scattered")
        s_cv = sem("a_convert")
        s_tab = sem("a_table")
        s_cnt = sem("a_counts")
        s_cp = sem("a_consts_pool")
        s_late = sem("a_late_consts")
        s_tb = sem("a_table_step")
        s_ex = sem("a_exp")
        s_fill = sem("a_filled")
        RT = 17

        block = ctx.enter_context(nc.Block())

        def preact(i, t):
            return xw[i][t % 2][:, (t // 2) * 4:(t // 2) * 4 + 4]

        @block.sync
        def _(sp):
            sp.dma_start(wx_sb[:], wx.rearrange("(k p) n -> p k n", p=P)).then_inc(s_w, 16)
            sp.dma_start(wh_sb, wh.rearrange("(k p) n -> p k n", p=P)).then_inc(s_w, 16)
            sp.dma_start(b_sb[:], bias).then_inc(s_w, 16)
            sp.dma_start(h0[:], h0T).then_inc(s_w, 16)
            sp.dma_start(gate_sb, gateT).then_inc(s_w, 16)
            for i in range(2):
                sp.dma_start(xt[:, i], xT[:, :, i * P:(i + 1) * P]).then_inc(s_x[i], 16)

            def load_x(blk, i, count):
                sp.wait_ge(s_xw, count)
                sp.dma_start(xt[:, i], xT[:, :, bass.ds(blk * P, P)]).then_inc(s_x[i], 16)

            def load_w(c, cc):
                if isinstance(c, int) and c < 2:
                    sp.wait_ge(s_prep, 6)
                else:
                    sp.wait_ge(s_cv, 3 * c - 3)
                sp.dma_start(stage[:, cc % 2], w_cols[:, bass.ds(c * CHUNK, CHUNK)]).then_inc(s_wst[cc % 2], 16)

            def pair(pr, last=False):
                for cc in range(CH_PAIR):
                    load_w(pr * CH_PAIR + cc, cc)
                    if cc in (1, CH_PAIR // 2 + 1) and not last:
                        i = cc // (CH_PAIR // 2)
                        load_x(pr * 2 + 2 + i, i, pr * 2 + 1 + i)

            pair(0)
            with sp.Fori(1, PAIRS - 1) as pr:
                pair(pr)
            pair(PAIRS - 1, last=True)
            sp.wait_ge(s_tab, 1)
            sp.wait_ge(s_late, 4)
            for e in range(E):
                n = sp.value_load(cnt_i[0:1, e:e + 1], min_val=0, max_val=REGION - P)
                sp.dma_start(rows_dram[bass.ds(n + e * REGION, P), :], zero_rows).then_inc(s_fill, 16)
            for j in range(MINT, MAXT):
                sp.dma_start(y_dram[j * P:(j + 1) * P, :], zero_rows.bitcast(F32)).then_inc(s_fill, 16)
            sp.wait_ge(s_fill, 16 * (E + MAXT - MINT))

        @block.tensor
        def _(pe):
            def xw_mm(i, q):
                p, m, k = q // 6, (q // 3) % 2, q % 3
                dst = xw[i][p][:, 0:P].rearrange("p (t c b) -> p t c b", c=2, b=B)[:, :, m, :]
                flags = dict(start=(m == 0 and k == 0), stop=False, skip_group_check=True)
                if k == 0:
                    return pe.matmul(dst, b_sb[0:1, m * P:(m + 1) * P], ones[0:1, :], **flags)
                mv = xt[:, i, k - 1, :].rearrange("p (t a b) -> p t a b", a=2, b=B)[:, :, p, :]
                return pe.matmul(dst, wx_sb[:, k - 1, m * P:(m + 1) * P], mv, **flags)

            def route(i, gi, tt):
                if tt == 1:
                    if not (isinstance(gi, int) and gi == 0):
                        pe.wait_ge(s_rt, gi * RT)
                    n = 0
                    for k in range(2):
                        for hp, gp in ((hi, gate_hi), (hi, gate_lo), (lo, gate_hi)):
                            mm = pe.matmul(p_lg[:, 0:E], hp[:, i, k, :], gp[:, k, :], start=(n == 0), stop=(n == 5))
                            n += 1
                    mm.then_inc(s_lg, 1)
                if tt in (3, 5):
                    if tt == 3 and not (isinstance(gi, int) and gi == 0):
                        pe.wait_ge(s_rows, gi * 4)
                    src = hi if tt == 3 else lo
                    for k in range(2):
                        c = (0 if tt == 3 else H) + k * P
                        mm = pe.transpose(p_rows[:, c:c + P], src[:, i, k, :], ident16[:])
                    mm.then_inc(s_tr, 1)
                if tt == 15:
                    pe.wait_ge(s_rt, gi * RT + 11)
                    pe.matmul(p_rank[:, 0:E], tri[:], chosen[:], start=True, stop=False)
                    pe.matmul(p_rank[:, 0:E], all1[:], seen[:, i, :], start=False, stop=True).then_inc(s_rk, 1)

            def step(pr, t, first, last):
                i, tt = t // STEPS, t % STEPS
                n = pr * WIN + t
                prev = (t - 1) % WIN
                pi, pt = prev // STEPS, prev % STEPS
                pe.wait_ge(s_hi, n + 1)
                for w in (wh_hi, wh_lo):
                    for m in range(2):
                        for k in range(2):
                            pe.matmul(preact(i, tt)[:, B * m:B * m + B], w[:, k, m * P:(m + 1) * P],
                                      hi[:, pi, k, B * pt:B * pt + B], start=False, stop=False, skip_group_check=True)
                pe.wait_ge(s_lo, n + 1)
                for m in range(2):
                    for k in range(2):
                        mm = pe.matmul(preact(i, tt)[:, B * m:B * m + B], wh_hi[:, k, m * P:(m + 1) * P],
                                       lo[:, pi, k, B * pt:B * pt + B], start=False, stop=False, skip_group_check=True)
                mm.then_inc(s_pre, 1)
                if tt % 4 == 2 and tt // 4 < 12 and not (last and i == 1):
                    if tt == 2:
                        pe.wait_ge(s_x[1 - i], 16 * (pr + 1 + i))
                    mm = xw_mm(1 - i, tt // 4)
                    if tt // 4 == 11:
                        mm.then_inc(s_xw, 1)
                if not (first and i == 0):
                    route(1 - i, pr * 2 + i - 1, tt)

            pe.wait_ge(s_prep, 6)
            pe.wait_ge(s_cst, 3)
            pe.wait_ge(s_cp, 5)
            pe.wait_ge(s_x[0], 16)
            for q in range(12):
                mm = xw_mm(0, q)
            mm.then_inc(s_xw, 1)
            for t in range(WIN):
                step(0, t, True, False)
            with pe.Fori(1, PAIRS - 1) as pr:
                for t in range(WIN):
                    step(pr, t, False, False)
            for t in range(WIN):
                step(PAIRS - 1, t, False, True)
            pe.wait_ge(s_hi, T + 1)
            pe.wait_ge(s_lo, T + 1)
            for tt in (1, 3, 5, 15):
                route(1, NBLK - 1, tt)
            pe.wait_ge(s_rt, NBLK * RT)
            pe.matmul(p_lg[:, 0:E], all1[:], seen[:, 0, :], start=True, stop=True).then_inc(s_cnt, 1)

        @block.scalar
        def _(act):
            def route(gi, tt):
                if 6 <= tt < 10:
                    q = tt - 6
                    act.wait_ge(s_tr, gi * 2 + 2)
                    if q == 0 and not (isinstance(gi, int) and gi == 0):
                        act.wait_ge(s_sc, gi * 32)
                    act.copy(rows[:, q * P:(q + 1) * P], p_rows[:, q * P:(q + 1) * P]).then_inc(s_rows, 1)

            def step(pr, t, first):
                i, tt = t // STEPS, t % STEPS
                n = pr * WIN + t
                act.wait_ge(s_pre, n + 1)
                src = preact(i, tt).rearrange("p (c b) -> p c b", c=2)
                act.activation(hi[:, i, :, B * tt:B * tt + B], src, ACT.Tanh, scale=1 / SCALE).then_inc(s_hi, 1)
                act.activation(h32[:, 4 * (t % 2):4 * (t % 2) + 4], preact(i, tt), ACT.Tanh,
                               scale=1 / SCALE).then_inc(s_h32, 1)
                if not (first and i == 0):
                    route(pr * 2 + i - 1, tt)

            act.wait_ge(s_w, 80)
            act.copy(hi[:, 1, :, P - B:P], h0[:]).then_inc(s_hi, 1)
            for t in range(WIN):
                step(0, t, True)
            with act.Fori(1, PAIRS) as pr:
                for t in range(WIN):
                    step(pr, t, False)
            for tt in range(6, 10):
                route(NBLK - 1, tt)
            act.wait_ge(s_tb, 1)
            act.activation(probs[:, 1, :], probs[:, 0, :], ACT.Exp, scale=1 / SCALE).then_inc(s_ex, 1)

        @block.vector
        def _(v):
            def done(gi, k):
                v.wait_ge(s_rt, gi * RT + k)

            def route(i, gi, tt):
                k = tt - 3
                if k == 0:
                    v.wait_ge(s_lg, gi + 1)
                    o = v.tensor_copy(lg[:], p_lg[:, 0:E])
                elif k == 1:
                    done(gi, 1)
                    o = v.tensor_reduce(st[:, 0:1], lg[:], AX.X, ALU.max)
                elif k == 2:
                    done(gi, 2)
                    o = v.scalar_tensor_tensor(out=pick[:], in0=lg[:], scalar=st[:, 0:1], in1=rev[:],
                                               op0=ALU.is_equal, op1=ALU.mult)
                elif k == 3:
                    done(gi, 3)
                    o = v.tensor_reduce(r1[:], pick[:], AX.X, ALU.max)
                elif k == 4:
                    done(gi, 4)
                    o = v.tensor_scalar(oh1[:], rev[:], r1[:, 0:1], None, ALU.is_equal)
                elif k == 5:
                    done(gi, 5)
                    o = v.scalar_tensor_tensor(out=lg2[:], in0=oh1[:], scalar=NEG, in1=lg[:],
                                               op0=ALU.mult, op1=ALU.add)
                elif k == 6:
                    done(gi, 6)
                    o = v.tensor_reduce(st[:, 1:2], lg2[:], AX.X, ALU.max)
                elif k == 7:
                    done(gi, 7)
                    o = v.scalar_tensor_tensor(out=pick[:], in0=lg2[:], scalar=st[:, 1:2], in1=rev[:],
                                               op0=ALU.is_equal, op1=ALU.mult)
                elif k == 8:
                    done(gi, 8)
                    o = v.tensor_reduce(r1[:], pick[:], AX.X, ALU.max)
                elif k == 9:
                    done(gi, 9)
                    o = v.tensor_scalar(oh2[:], rev[:], r1[:, 0:1], None, ALU.is_equal)
                elif k == 10:
                    done(gi, 10)
                    o = v.tensor_tensor(chosen[:], oh1[:], oh2[:], ALU.add)
                elif k == 11:
                    done(gi, 11)
                    o = v.tensor_tensor(seen[:, 1 - i, :], seen[:, i, :], chosen[:], ALU.add)
                elif k == 14:
                    v.wait_ge(s_rk, gi + 1)
                    o = v.tensor_tensor(rank[:], p_rank[:, 0:E], base[:], ALU.add)
                elif k == 15:
                    done(gi, 13)
                    o = v.tensor_tensor_reduce(pick[:], oh1[:], rank[:], 1.0, 0.0, ALU.mult, ALU.add, st[:, 2:3])
                elif k == 16:
                    done(gi, 14)
                    o = v.tensor_tensor_reduce(pick[:], oh2[:], rank[:], 1.0, 0.0, ALU.mult, ALU.add, st[:, 3:4])
                elif k == 17:
                    done(gi, 15)
                    v.wait_ge(s_rows, gi * 4 + 4)
                    if not (isinstance(gi, int) and gi == 0):
                        v.wait_ge(s_sc, gi * 32)
                    o = v.tensor_copy(slot[:], st[:, 2:4])
                elif k == 18:
                    done(gi, 16)
                    dst = stats[:, gi, :] if isinstance(gi, int) else stats[:, bass.ds(gi, 1), :].rearrange("p a c -> p (a c)")
                    o = v.tensor_copy(dst, st[:])
                else:
                    return
                o.then_inc(s_rt, 1)

            def step(pr, t, first):
                i, tt = t // STEPS, t % STEPS
                n = pr * WIN + t
                v.wait_ge(s_h32, n + 1)
                v.tensor_tensor(lo[:, i, :, B * tt:B * tt + B],
                                h32[:, 4 * (t % 2):4 * (t % 2) + 4].rearrange("p (c b) -> p c b", c=2),
                                hi[:, i, :, B * tt:B * tt + B], ALU.subtract).then_inc(s_lo, 1)
                if not (first and i == 0):
                    route(1 - i, pr * 2 + i - 1, tt)

            v.memset(ones[:], 1.0).then_inc(s_cst, 1)
            v.memset(all1[:], 1.0).then_inc(s_cst, 1)
            v.memset(seen[:], 0.0).then_inc(s_cst, 1)
            v.wait_ge(s_w, 80)
            v.tensor_scalar(wh_hi[:], wh_sb, SCALE, None, ALU.mult).then_inc(s_prep, 1)
            v.tensor_scalar(gate_hi[:], gate_sb, SCALE, None, ALU.mult).then_inc(s_prep, 1)
            v.tensor_scalar(wx_sb[:], wx_sb[:], SCALE, None, ALU.mult).then_inc(s_prep, 1)
            v.tensor_scalar(b_sb[:], b_sb[:], SCALE, None, ALU.mult).then_inc(s_prep, 1)
            v.wait_ge(s_prep, 4)
            v.scalar_tensor_tensor(out=wh_lo[:], in0=wh_sb, scalar=SCALE, in1=wh_hi[:],
                                   op0=ALU.mult, op1=ALU.subtract).then_inc(s_prep, 1)
            v.scalar_tensor_tensor(out=gate_lo[:], in0=gate_sb, scalar=SCALE, in1=gate_hi[:],
                                   op0=ALU.mult, op1=ALU.subtract).then_inc(s_prep, 1)
            v.wait_ge(s_hi, 1)
            v.tensor_tensor(lo[:, 1, :, P - B:P], h0[:], hi[:, 1, :, P - B:P], ALU.subtract).then_inc(s_lo, 1)
            v.wait_ge(s_cp, 5)
            for t in range(WIN):
                step(0, t, True)
            with v.Fori(1, PAIRS) as pr:
                for t in range(WIN):
                    step(pr, t, False)
            for tt in range(3, 22):
                route(1, NBLK - 1, tt)

            steps_done = [0]

            def link(o):
                steps_done[0] += 1
                o.then_inc(s_tb, 1)
                v.wait_ge(s_tb, steps_done[0])

            v.wait_ge(s_rt, NBLK * RT)
            link(v.tensor_tensor(probs[:, 0, :], stats[:, :, 1], stats[:, :, 0], ALU.subtract))
            v.wait_ge(s_ex, 1)
            link(v.tensor_scalar(probs[:, 0, :], probs[:, 1, :], 1.0, None, ALU.add))
            link(v.reciprocal(probs[:, 0, :], probs[:, 0, :]))
            link(v.tensor_tensor(probs[:, 1, :], probs[:, 1, :], probs[:, 0, :], ALU.mult))

            v.wait_ge(s_cnt, 1)
            v.wait_ge(s_late, 4)
            link(v.tensor_copy(cnt, p_lg[:, 0:E]))
            v.tensor_copy(cnt_i, cnt).then_inc(s_tab, 1)
            q3 = cmp[:, 0:E * NBLK].rearrange("p (e q) -> p e q", e=E)
            link(v.tensor_tensor(q3, cnt.unsqueeze(2).to_broadcast([P, E, NBLK]),
                                 qrow.unsqueeze(1).to_broadcast([P, E, NBLK]), ALU.is_gt))
            link(v.tensor_reduce(nt, q3, AX.X, ALU.add))
            e3 = cmp[:, 0:E * E].rearrange("p (e q) -> p e q", e=E)
            link(v.tensor_tensor(e3, tri8, nt.unsqueeze(1).to_broadcast([P, E, E]), ALU.mult))
            link(v.tensor_reduce(end, e3, AX.X, ALU.add))
            j3 = cmp.rearrange("p (j e) -> p j e", e=E)
            link(v.tensor_tensor(j3, jrow.unsqueeze(2).to_broadcast([P, MAXT + 1, E]),
                                 end.unsqueeze(1).to_broadcast([P, MAXT + 1, E]), ALU.is_ge))
            link(v.tensor_reduce(ej, j3, AX.X, ALU.add))
            link(v.tensor_tensor(j3, j3, nt.unsqueeze(1).to_broadcast([P, MAXT + 1, E]), ALU.mult))
            link(v.tensor_reduce(sj, j3, AX.X, ALU.add))
            link(v.tensor_tensor(sj, jrow, sj, ALU.subtract))
            link(v.tensor_scalar(sj, sj, float(P), None, ALU.mult))
            link(v.scalar_tensor_tensor(out=sj, in0=ej, scalar=float(REGION), in1=sj, op0=ALU.mult, op1=ALU.add))
            link(v.tensor_copy(table[:, 0, :], ej[0:1, :]))
            link(v.tensor_copy(table[:, 1, :], sj[0:1, :]))
            link(v.tensor_scalar(ntiles[:], end[0:1, E - 1:E], -2.0, None, ALU.add))
            link(v.tensor_copy(slots.rearrange("p (k g) -> p k g", k=2), stats[:, :, 2:4].rearrange("p g k -> p k g")))
            link(v.tensor_scalar(cnt[:, 0:E - 1], nt[:, 0:E - 1], -float(P), float(REGION), ALU.mult, ALU.add))
            g3 = cmp[:, 0:2 * NBLK * (E - 1)].rearrange("p (s e) -> p s e", e=E - 1)
            link(v.tensor_tensor(g3, slots.unsqueeze(2).to_broadcast([P, 2 * NBLK, E - 1]),
                                 base[:, 1:E].unsqueeze(1).to_broadcast([P, 2 * NBLK, E - 1]), ALU.is_ge))
            link(v.tensor_tensor(g3, g3, cnt[:, 0:E - 1].unsqueeze(1).to_broadcast([P, 2 * NBLK, E - 1]), ALU.mult))
            link(v.tensor_reduce(moved, g3, AX.X, ALU.add))
            link(v.tensor_tensor(places[:].rearrange("p k g -> p (k g)"), slots, moved, ALU.subtract))

        @block.gpsimd
        def _(pool):
            pool.memset(ident32[:], 0.0).then_inc(s_cp, 1)
            pool.memset(tri[:], 1.0).then_inc(s_cp, 1)
            pool.wait_ge(s_cp, 2)
            pool.affine_select(out=ident32[:], in_=ident32[:], compare_op=ALU.not_equal, fill=1.0, base=0,
                               pattern=[[-1, P]], channel_multiplier=1).then_inc(s_cp, 1)
            pool.affine_select(out=tri[:], in_=tri[:], compare_op=ALU.is_gt, fill=0.0, base=0,
                               pattern=[[1, P]], channel_multiplier=-1)
            pool.iota(rev[:], [[-1, E]], base=E, channel_multiplier=0, allow_small_or_imprecise_dtypes=True)
            pool.iota(base[:], [[REGION, E]], base=0, channel_multiplier=0,
                      allow_small_or_imprecise_dtypes=True).then_inc(s_cp, 1)
            pool.wait_ge(s_cp, 4)
            pool.tensor_copy(ident16[:], ident32[:]).then_inc(s_cp, 1)

            loaded = pool.alloc_register("loaded")
            routed = pool.alloc_register("routed")
            pool.reg_mov(loaded, 16)
            pool.reg_mov(routed, 16)

            def convert(pr, cc):
                c = pr * CH_PAIR + cc
                src = stage[:, cc % 2, :]
                pool.wait_ge(s_prep, 6)
                pool.wait_ge(s_wst[cc % 2], loaded)
                cols = bass.ds(c * CHUNK, CHUNK)
                pool.tensor_scalar(src, src, SCALE, None, ALU.mult).then_inc(s_cv, 1)
                if cc % 2:
                    pool.reg_add(loaded, loaded, 16)
                pool.wait_ge(s_cv, 3 * c + 1)
                pool.tensor_copy(w_hi_cols[:, cols], src).then_inc(s_cv, 1)
                pool.wait_ge(s_cv, 3 * c + 2)
                pool.tensor_tensor(w_lo_cols[:, cols], src, w_hi_cols[:, cols], ALU.subtract).then_inc(s_cv, 1)

            def scatter():
                pool.wait_ge(s_cp, 5)
                pool.wait_ge(s_rt, routed)
                for k in range(2):
                    pool.indirect_dma_start(rows_dram, bass.IndirectOffsetOnAxis(ap=slot[:, k:k + 1], axis=0),
                                            rows[:], None).then_inc(s_sc, 16)
                pool.reg_add(routed, routed, RT)

            def pair(pr, first=False):
                for cc in range(CH_PAIR):
                    convert(pr, cc)
                    if cc == CH_PAIR // 2 - 1 and not first:
                        scatter()
                scatter()

            pair(0, first=True)
            with pool.Fori(1, PAIRS) as pr:
                pair(pr)
            pool.wait_ge(s_cv, 3 * CH_PAIR * PAIRS)
            pool.wait_ge(s_xw, NBLK)
            pool.memset(zero_rows, 0.0).then_inc(s_late, 1)
            pool.memset(tri8, 1.0).then_inc(s_late, 1)
            pool.wait_ge(s_late, 2)
            pool.affine_select(out=tri8, in_=tri8, compare_op=ALU.is_ge, fill=0.0, base=0,
                               pattern=[[1, E], [-1, E]], channel_multiplier=0).then_inc(s_late, 1)
            pool.iota(qrow, [[P, NBLK]], base=0, channel_multiplier=0, allow_small_or_imprecise_dtypes=True)
            pool.iota(jrow, [[1, MAXT + 1]], base=0, channel_multiplier=0,
                      allow_small_or_imprecise_dtypes=True).then_inc(s_late, 1)
            scatter()
            pool.wait_ge(s_sc, 32 * NBLK)


def experts(nc, g):
    rows_dram, y_dram, w_hi, w_lo = g["rows_dram"], g["y_dram"], g["w_hi"], g["w_lo"]
    ident32, ident16, table, ntiles = (g[k] for k in ("ident32", "ident16", "table", "ntiles"))
    H, E, KC, INNER, IC, GU, REGION, ROW = (g[k] for k in ("H", "E", "KC", "INNER", "IC", "GU", "REGION", "ROW"))
    MAXT, MINT = g["MAXT"], g["MINT"]
    HALF = INNER // 2

    with ExitStack() as ctx:
        def sb(name, shape, dt):
            return ctx.enter_context(nc.sbuf_tensor(name, shape, dt))

        def ps(name, shape, dt):
            return ctx.enter_context(nc.psum_tensor(name, shape, dt))

        def sem(name):
            return ctx.enter_context(nc.semaphore(name))

        xrow = sb("xrow", [P, ROW], F16)
        xT = sb("xTt", [P, 2 * KC, P], F16)
        hid = sb("hid", [P, INNER], F32)
        hT_hi = sb("hT_hi", [P, IC, P], F16)
        hT_lo = sb("hT_lo", [P, IC, P], F16)
        y_sb = sb("y_sb", [P, H], F32)
        p_g = [ps(f"p_g{h}", [P, HALF], F32) for h in range(2)]
        p_u = [ps(f"p_u{h}", [P, HALF], F32) for h in range(2)]
        p_h = [ps(f"p_h{h}", [P, HALF], F32) for h in range(2)]
        p_x = ps("p_x", [P, 2 * ROW], F16)
        p_y = ps("p_y", [P, HALF], F32)

        s_xrow = sem("b_rows_in")
        s_xtp = sem("b_xT_psum")
        s_xt = sem("b_xT")
        s_g = sem("b_gate")
        s_u = sem("b_up")
        s_sil = sem("b_silu")
        s_hid = sem("b_hidden")
        s_th = sem("b_hidden_T")
        s_hhi = sem("b_hT_hi")
        s_hlo = sem("b_hT_lo")
        s_d = sem("b_down")
        s_y = sem("b_y_sb")
        s_yout = sem("b_y_out")
        s_ylast = sem("b_y_out_last")

        block = ctx.enter_context(nc.Block())

        def tiles(eng):
            return eng.value_load(ntiles[0:1, 0:1], min_val=MINT - 2, max_val=MAXT - 2)

        def entry(eng, which, j, hi):
            a = table[0:1, which, j:j + 1] if isinstance(j, int) else table[0:1, which, bass.ds(j, 1)]
            return eng.value_load(a, min_val=0, max_val=hi)

        @block.sync
        def _(sp):
            m = tiles(sp)

            def load(j):
                row = entry(sp, 1, j, E * REGION - P)
                sp.dma_start(xrow[:], rows_dram[bass.ds(row, P), :]).then_inc(s_xrow, 16)

            def store(j, s=s_yout):
                sp.wait_ge(s_y, j + 1)
                sp.dma_start(y_dram[bass.ds(j * P, P), :], y_sb[:]).then_inc(s, 16)

            load(0)
            sp.wait_ge(s_xtp, 1)
            load(1)
            with sp.Fori(1, m + 1) as j:
                sp.wait_ge(s_xtp, j + 1)
                load(j + 1)
                store(j - 1)
            store(m)
            store(m + 1, s_ylast)
            sp.wait_ge(s_ylast, 16)

        @block.tensor
        def _(pe):
            m = tiles(pe)

            def turn_x(j):
                pe.wait_ge(s_xrow, 16 * (j + 1))
                for c in range(2 * KC):
                    mm = pe.transpose(p_x[:, c * P:(c + 1) * P], xrow[:, c * P:(c + 1) * P], ident16[:])
                mm.then_inc(s_xtp, 1)

            def gate_up(j, first=False):
                e = entry(pe, 0, j, E - 1)
                pe.wait_ge(s_xt, j + 1)
                if not first:
                    pe.wait_ge(s_hid, 2 * j)
                for h in range(2):
                    for which, dst, s in ((0, p_g[h], s_g), (1, p_u[h], s_u)):
                        q = 0
                        for k in range(KC):
                            at = k * 2 * INNER + which * INNER + h * HALF
                            for xpart, w in ((k, w_hi), (KC + k, w_hi), (k, w_lo)):
                                rhs = w[:, bass.ds(e, 1), at:at + HALF].rearrange("p a c -> p (a c)")
                                mm = pe.matmul(dst[:], xT[:, xpart, :], rhs, start=(q == 0), stop=(q == 3 * KC - 1))
                                q += 1
                        mm.then_inc(s, 1)

            def down(j, first=False):
                e = entry(pe, 0, j, E - 1)
                pe.wait_ge(s_hlo, 2 * (j + 1))
                if not first:
                    pe.wait_ge(s_y, j)
                q = 0
                for c in range(IC):
                    for hp, w in ((hT_hi, w_hi), (hT_hi, w_lo), (hT_lo, w_hi)):
                        rhs = w[:, bass.ds(e, 1), GU + c * H:GU + (c + 1) * H].rearrange("p a c -> p (a c)")
                        mm = pe.matmul(p_y[:, 0:H], hp[:, c, :], rhs, start=(q == 0), stop=(q == 3 * IC - 1))
                        q += 1
                mm.then_inc(s_d, 1)

            def turn_hidden(j):
                for h in range(2):
                    pe.wait_ge(s_hid, 2 * j + 1 + h)
                    for c in range(IC // 2):
                        mm = pe.transpose(p_h[h][:, c * P:(c + 1) * P],
                                          hid[:, h * HALF + c * P:h * HALF + (c + 1) * P], ident32[:])
                    mm.then_inc(s_th, 1)

            turn_x(0)
            gate_up(0, first=True)
            turn_x(1)
            turn_hidden(0)
            gate_up(1)
            turn_x(2)
            down(0, first=True)
            turn_hidden(1)
            with pe.Fori(2, m + 1) as j:
                gate_up(j)
                turn_x(j + 1)
                down(j - 1)
                turn_hidden(j)
            gate_up(m + 1)
            down(m)
            turn_hidden(m + 1)
            down(m + 1)

        @block.scalar
        def _(act):
            m = tiles(act)

            def x_out(j):
                act.wait_ge(s_xtp, j + 1)
                act.copy(xT[:].rearrange("p c t -> p (c t)"), p_x[:, 0:ROW]).then_inc(s_xt, 1)

            def silu(j, first=False):
                for h in range(2):
                    act.wait_ge(s_g, 2 * j + 1 + h)
                    if not first:
                        act.wait_ge(s_th, 2 * j)
                    act.activation(hid[:, h * HALF:(h + 1) * HALF], p_g[h][:], ACT.Silu,
                                   scale=1 / SCALE).then_inc(s_sil, 1)

            def hidden_hi(j):
                for h in range(2):
                    act.wait_ge(s_th, 2 * j + 1 + h)
                    act.copy(hT_hi[:, h * (IC // 2):(h + 1) * (IC // 2), :].rearrange("p c t -> p (c t)"),
                             p_h[h][:]).then_inc(s_hhi, 1)

            def y_scale(j, first=False):
                act.wait_ge(s_d, j + 1)
                if not first:
                    act.wait_ge(s_yout, 16 * j)
                act.mul(y_sb[:], p_y[:, 0:H], 1 / SCALE).then_inc(s_y, 1)

            x_out(0)
            silu(0, first=True)
            x_out(1)
            hidden_hi(0)
            silu(1)
            x_out(2)
            y_scale(0, first=True)
            hidden_hi(1)
            with act.Fori(2, m + 1) as j:
                silu(j)
                x_out(j + 1)
                y_scale(j - 1)
                hidden_hi(j)
            silu(m + 1)
            y_scale(m)
            hidden_hi(m + 1)
            y_scale(m + 1)

        @block.vector
        def _(v):
            m = tiles(v)

            def times_up(j):
                for h in range(2):
                    v.wait_ge(s_sil, 2 * j + 1 + h)
                    v.wait_ge(s_u, 2 * j + 1 + h)
                    part = hid[:, h * HALF:(h + 1) * HALF]
                    v.scalar_tensor_tensor(out=part, in0=p_u[h][:], scalar=1 / SCALE, in1=part,
                                           op0=ALU.mult, op1=ALU.mult).then_inc(s_hid, 1)

            def hidden_lo(j):
                for h in range(2):
                    v.wait_ge(s_hhi, 2 * j + 1 + h)
                    cs = slice(h * (IC // 2), (h + 1) * (IC // 2))
                    v.tensor_tensor(hT_lo[:, cs, :].rearrange("p c t -> p (c t)"), p_h[h][:],
                                    hT_hi[:, cs, :].rearrange("p c t -> p (c t)"), ALU.subtract).then_inc(s_hlo, 1)

            with v.Fori(0, m + 2) as j:
                times_up(j)
                hidden_lo(j)


def combine(nc, g):
    x, out, y_dram, probs, places = (g[k] for k in ("x", "out", "y_dram", "probs", "places"))
    H, NBLK, STEPS = g["H"], g["NBLK"], g["STEPS"]

    with ExitStack() as ctx:
        def sb(name, shape, dt):
            return ctx.enter_context(nc.sbuf_tensor(name, shape, dt))

        def sem(name):
            return ctx.enter_context(nc.semaphore(name))

        x_sb = sb("x_sb", [P, NBLK, H], F32)
        yg = sb("yg", [P, NBLK, 2, H], F32)
        s_in = [sem(f"c_in{n}") for n in range(NBLK)]
        s_x = sem("c_x_in")
        s_one = sem("c_first")
        s_sum = sem("c_sum")
        s_out = sem("c_out")
        block = ctx.enter_context(nc.Block())

        def tokens(a, n):
            return a[:, n * STEPS:(n + 1) * STEPS, :].rearrange("b t d -> t b d")

        @block.sync
        def _(sp):
            for n in range(NBLK):
                sp.dma_start(x_sb[:, n, :], tokens(x, n)).then_inc(s_x, 16)
            for n in range(NBLK):
                sp.wait_ge(s_sum, n + 1)
                sp.dma_start(tokens(out, n), x_sb[:, n, :]).then_inc(s_out, 16)
            sp.wait_ge(s_out, 16 * NBLK)

        @block.gpsimd
        def _(pool):
            for n in range(NBLK):
                for k in range(2):
                    pool.indirect_dma_start(yg[:, n, k, :], None, y_dram,
                                            bass.IndirectOffsetOnAxis(ap=places[:, k, n:n + 1], axis=0)
                                            ).then_inc(s_in[n], 16)

        @block.vector
        def _(v):
            v.wait_ge(s_x, 16 * NBLK)
            for n in range(NBLK):
                v.wait_ge(s_in[n], 32)
                v.scalar_tensor_tensor(out=x_sb[:, n, :], in0=yg[:, n, 0, :], scalar=probs[:, 0, n:n + 1],
                                       in1=x_sb[:, n, :], op0=ALU.mult, op1=ALU.add).then_inc(s_one, 1)
                v.wait_ge(s_one, n + 1)
                v.scalar_tensor_tensor(out=x_sb[:, n, :], in0=yg[:, n, 1, :], scalar=probs[:, 1, n:n + 1],
                                       in1=x_sb[:, n, :], op0=ALU.mult, op1=ALU.add).then_inc(s_sum, 1)


def kernel(x, cond_1024, L0_cond_Wx, L0_cond_Wh, L0_cond_b, L0_ffn_gate_w, L0_ffn_wg, L0_ffn_wu, L0_ffn_wd):
    import concourse.bacc as bacc
    import numpy as np
    from concourse.bass_utils import run_bass_kernel_spmd

    a = np.asarray
    x = a(x)
    b, t, d = x.shape
    e, inner, _ = L0_ffn_wg.shape
    kc = d // P

    def chunks(m):
        return np.ascontiguousarray(m.reshape(kc, P, *m.shape[1:]).swapaxes(0, 1))

    wg = a(L0_ffn_wg).transpose(2, 0, 1).reshape(kc, P, e, 1, inner)
    wu = a(L0_ffn_wu).transpose(2, 0, 1).reshape(kc, P, e, 1, inner)
    gu = np.concatenate([wg, wu], axis=3).transpose(1, 2, 0, 3, 4).reshape(P, e, -1)
    dn = a(L0_ffn_wd).transpose(2, 0, 1).reshape(inner // P, P, e, d).transpose(1, 2, 0, 3).reshape(P, e, -1)
    arrays = {
        "xT": chunks(x.transpose(2, 1, 0).reshape(d, t * b)),
        "x_in": np.ascontiguousarray(x),
        "h0T": chunks(a(cond_1024).T),
        "wx_in": np.ascontiguousarray(a(L0_cond_Wx)),
        "wh_in": np.ascontiguousarray(a(L0_cond_Wh)),
        "bias_in": np.ascontiguousarray(a(L0_cond_b)).reshape(1, -1),
        "gateT": chunks(a(L0_ffn_gate_w).T),
        "w_all": np.ascontiguousarray(np.concatenate([gu, dn], axis=2)),
    }
    nc = bacc.Bacc("TRN2", target_bir_lowering=False, num_devices=1)
    args = [nc.dram_tensor(k, v.shape, mybir.dt.from_np(v.dtype), kind="ExternalInput").ap() for k, v in arrays.items()]
    out = nc.dram_tensor("out", x.shape, F32, kind="ExternalOutput").ap()
    build(nc, *args, out)
    result = run_bass_kernel_spmd(nc, [arrays], core_ids=[0])
    return result.results[0]["out"]
```

```python
from contextlib import ExitStack

import concourse.bass as bass
from concourse import mybir

F32 = mybir.dt.float32
F16 = mybir.dt.float16
I32 = mybir.dt.int32
ALU = mybir.AluOpType
ACT = mybir.ActivationFunctionType
AX = mybir.AxisListType

P = 128
SCALE = 16.0
NEG = -3.0e38
PAD = 8

G_AT, U_AT = (8, 14), (11, 17)
SILU_AT, MUL_AT = (11, 17), (14, 20)
TURN_AT, HI_AT, LO_AT = (20, 23), (21, 24), (22, 25)
DOWN_AT, Y_AT = 26, 32
TILE_B = 24
TURN_X_AT, X_OUT_AT = (57, 21), (58, 22)
TAKE_AT, SHIFT_AT = (58, 24), (63, 48)
XW_AT = ((3, 5, 7, 25, 45, 49), (4, 22, 24, 46, 48, 56))
UPDATE_AT = (26, 27, 28, 29, 30, 31, 32, 33, 34, 35, 36, 37, 39, 40, 41, 42, 43, 45, 47, 50, 51, 52)
FIRST = 4


def build(nc, xT, x, h0T, wx, wh, bias, gateT, w_all, tok0, out):
    B, T, D = x.shape
    H = wh.shape[0]
    E = gateT.shape[2]
    KC = H // P
    TOK = B * T
    STEPS = P // B
    NBLK = T // STEPS
    PAIRS = NBLK // 2
    WIN = 2 * STEPS
    WCOL = w_all.shape[2]
    INNER = WCOL // (3 * KC)
    HALF = INNER // 2
    IC = INNER // P
    HC = IC // 2
    GU = KC * 2 * INNER
    CHUNK = 512
    NCH = E * WCOL // CHUNK
    RING = 4
    REGION = TOK + P
    ROW = 2 * H
    ROWP = H + PAD
    WINDOW = 2 * E
    FQ = 2 * (NBLK - FIRST)
    LEAST = FQ + 4
    QMAX = FQ + 2 * TOK // P + E - 1
    NQ = QMAX + 2 * WINDOW
    RT = 21
    UP = len(UPDATE_AT)
    UP_FROM = 2
    assert KC == 2 and B == 2 and HALF == 512 and NCH <= STEPS + 36 and FIRST % 2 == 0

    rows_dram = nc.dram_tensor("expert_rows", (E * REGION + WINDOW * P, ROWP), F32, kind="Internal").ap()
    acc = nc.dram_tensor("accumulated", (TOK + P, H), F32, kind="Internal").ap()
    w_cols = w_all.rearrange("p e c -> p (e c)")

    with ExitStack() as ctx:
        def sb(name, shape, dt):
            return ctx.enter_context(nc.sbuf_tensor(name, shape, dt))

        def ps(name, shape, dt):
            return ctx.enter_context(nc.psum_tensor(name, shape, dt))

        def sem(name):
            return ctx.enter_context(nc.semaphore(name))

        w_hi = sb("w_hi", [P, E, WCOL], F16)
        w_lo = sb("w_lo", [P, E, WCOL], F16)
        w_hi_cols = w_hi[:].rearrange("p e c -> p (e c)")
        w_lo_cols = w_lo[:].rearrange("p e c -> p (e c)")
        ident32 = sb("ident32", [P, P], F32)
        ident16 = sb("ident16", [P, P], F16)
        tri = sb("tri", [P, P], F16)
        all1 = sb("all1", [P, P], F16)

        wx_sb = sb("wx_sb", [P, 2, H], F32)
        wh_hi = sb("wh_hi", [P, 2, H], F16)
        wh_lo = sb("wh_lo", [P, 2, H], F16)
        b_sb = sb("b_sb", [1, H], F32)
        ones = sb("ones", [1, STEPS], F32)
        h0 = sb("h0", [P, 2, B], F32)
        hi = sb("hi", [P, 2, 2, P], F16)
        lo = sb("lo", [P, 2, 2, P], F16)
        xt = sb("xt", [P, 2, 2, P], F32)

        gate_hi = sb("gate_hi", [P, 2, E], F16)
        gate_lo = sb("gate_lo", [P, 2, E], F16)
        rev = sb("rev", [P, E], F32)
        base = sb("base", [P, E], F32)
        seen = sb("seen", [P, 2, E], F16)
        lg = sb("lg", [P, E], F32)
        lg2 = sb("lg2", [P, E], F32)
        pick = sb("pick", [P, E], F32)
        oh1 = sb("oh1", [P, E], F32)
        oh2 = sb("oh2", [P, E], F32)
        chosen = sb("chosen", [P, E], F16)
        rank = sb("rank", [P, E], F32)
        st = sb("st", [P, 8], F32)
        slot = sb("slot", [P, 2], I32)
        tok = sb("tok", [P, 1], F32)
        rows = sb("rows", [P, 2, ROWP], F32)
        rows16 = rows[:, :, 0:H].bitcast(F16)
        meta = rows[:, :, H:H + 2]
        pad = sb("pad", [P, ROWP], F32)

        queue = sb("queue", [1, 2, NQ], I32)
        counts_i = sb("counts_i", [1, E], I32)
        small = sb("small", [1, 448], F32)
        cut, at = {}, 0
        for name, n in dict(cmp=P, cnt=E, full=E, new=E, upto=E, step=E, had=E + 1, place=1, floor=1, qi=1, left=1,
                            ej=WINDOW, sj=WINDOW, gj=WINDOW, irow=WINDOW, qrow=NBLK, frow=NBLK, tri8=E * E).items():
            cut[name] = small[0:1, at:at + n]
            at += n
        cmp, cnt, full, new, upto, step_e, had, place, floor, qi, left, ej, sj, gj, irow, qrow, frow, tri8 = cut.values()
        qi, left = qi.bitcast(I32), left.bitcast(I32)
        tri8 = tri8.rearrange("p (a b) -> p a b", a=E)

        xrow = sb("xrow", [P, ROWP], F32)
        xrow16 = xrow[:, 0:H].bitcast(F16)
        xrow_meta = xrow[:, H:H + 2]
        x_T = sb("x_T", [P, 2 * KC, P], F16)
        meta_in = sb("meta_in", [P, 2], F32)
        place_now = sb("place_now", [P, 1], I32)
        weight_now = sb("weight_now", [P, 1], F32)
        y_sb = sb("y_sb", [P, H], F32)
        arena = sb("arena", [P, 2 * INNER], F32)
        hid = arena[:, 0:INNER]
        hT_hi = arena[:, INNER:INNER + INNER // 2].bitcast(F16).rearrange("p (c t) -> p c t", c=IC)
        hT_lo = arena[:, INNER + INNER // 2:2 * INNER].bitcast(F16).rearrange("p (c t) -> p c t", c=IC)
        stage = arena[:].rearrange("p (a c) -> p a c", a=RING)
        wh_sb = stage[:, 0, :].rearrange("p (k n) -> p k n", k=2)
        gate_sb = stage[:, 1, 0:2 * E].rearrange("p (k e) -> p k e", k=2)

        bank = [ps(f"bank{n}", [P, 512], F32) for n in range(8)]
        xw = bank[0:2]
        h32 = bank[2]
        p_y = bank[6]
        misc = bank[7]
        p_x = misc[:, 0:ROW // 2].bitcast(F16)
        p_rows = p_x
        p_lg = misc[:, 0:E]
        p_rank = misc[:, 256:256 + E]
        p_cnt = misc[:, 320:320 + E]
        BETWEEN = dict(g=(bank[3], bank[3]), u=(bank[4], bank[4]), h=(bank[5], bank[5]))
        AFTER = dict(g=(bank[3], bank[0]), u=(bank[4], bank[1]), h=(bank[5], bank[2]))

        s_w = sem("weights_in")
        s_x = [sem("x_in0"), sem("x_in1")]
        s_st = [sem(f"stage_in{n}") for n in range(RING)]
        s_c = sem("consts_vector")
        s_cp = sem("consts_pool")
        s_padc = sem("pad_made")
        s_prep = sem("weights_split")
        s_xw = sem("xw_done")
        s_clr = sem("xw_cleared")
        s_pre = sem("preact")
        s_hi = sem("h_hi")
        s_h32 = sem("h_full")
        s_lo = sem("h_lo")
        s_lg = sem("logits")
        s_tr = sem("rows_turned")
        s_rows = sem("rows_copied")
        s_rt = sem("routed")
        s_tanh = sem("weight_tanh")
        s_rk = sem("ranks")
        s_sc = sem("rows_scattered")
        s_ch = sem("chunk_hi")
        s_cl = sem("chunk_lo")
        s_up = sem("queue_updated")
        s_fill = sem("padded")
        s_acc = sem("accumulator_started")
        s_xrow = sem("tile_in")
        s_xtp = sem("tile_turned")
        s_xt = sem("tile_T")
        s_g = sem("gate_done")
        s_u = sem("up_done")
        s_sil = sem("silu_done")
        s_hid = sem("hidden_done")
        s_th = sem("hidden_turned")
        s_hhi = sem("hT_hi_done")
        s_hlo = sem("hT_lo_done")
        s_d = sem("down_done")
        s_mt = sem("meta_moved")
        s_y = sem("y_ready")
        s_scat = sem("y_added")
        s_scat_last = sem("y_added_last")
        s_out = sem("out_written")

        block = ctx.enter_context(nc.Block())

        def preact(i, t):
            c = i * P + (t // 2) * 4
            return xw[t % 2][:, c:c + 4]

        def is0(v):
            return isinstance(v, int) and v == 0

        def entry(eng, which, q):
            a = queue[0:1, which, q:q + 1] if isinstance(q, int) else queue[0:1, which, bass.ds(q, 1)]
            return eng.value_load(a, min_val=0, max_val=(E - 1, E * REGION + (WINDOW - 1) * P)[which])

        def tiles_left(eng):
            return eng.value_load(left, min_val=0, max_val=QMAX - LEAST)

        def chunk_of(t):
            n = t if t < STEPS else (t - 28 if t >= STEPS + 28 else None)
            return n if n is not None and n < NCH else None

        def modes(pr, i):
            blk = pr * 2 + i if isinstance(pr, int) else None
            return dict(routes=blk != 0, tiles=blk is None or blk >= FIRST, ahead=blk is None or blk >= FIRST - 1,
                        last=blk == NBLK - 1)

        def tiles_last(eng):
            eng.wait_ge(s_up, UP * (NBLK - UP_FROM + 1) + 1)
            return tiles_left(eng)

        @block.sync
        def _(sp):
            sp.dma_start(wh_sb, wh.rearrange("(k p) n -> p k n", p=P)).then_inc(s_w, 16)
            sp.dma_start(wx_sb[:], wx.rearrange("(k p) n -> p k n", p=P)).then_inc(s_w, 16)
            sp.dma_start(b_sb[:], bias).then_inc(s_w, 16)
            sp.dma_start(h0[:], h0T).then_inc(s_w, 16)
            sp.dma_start(gate_sb, gateT).then_inc(s_w, 16)
            sp.dma_start(tok[:], tok0).then_inc(s_w, 16)
            for i in range(2):
                sp.dma_start(xt[:, i], xT[:, :, i * P:(i + 1) * P]).then_inc(s_x[i], 16)

            def load_x(blk, i):
                sp.wait_ge(s_xw, blk + 1)
                sp.dma_start(xt[:, i], xT[:, :, bass.ds((blk + 2) * P, P)]).then_inc(s_x[i], 16)

            def load_tile(q):
                if not is0(q):
                    sp.wait_ge(s_xtp, q)
                    sp.wait_ge(s_mt, 3 * q - 2)
                row = entry(sp, 1, q)
                sp.dma_start(xrow[:], rows_dram[bass.ds(row, P), :]).then_inc(s_xrow, 16)

            def load_tile_a(blk):
                sp.wait_ge(s_up, UP * (blk - UP_FROM + 1))
                sp.wait_ge(s_sc, scattered)
                sp.reg_add(scattered, scattered, 32)
                load_tile(2 * (blk + 1 - FIRST))

            scattered = sp.alloc_register("scattered_count")
            sp.reg_mov(scattered, 32 * (FIRST - 1))

            sp.wait_ge(s_prep, 6)
            for c in range(NCH):
                if c >= RING:
                    sp.wait_ge(s_cl, c - RING + 1)
                sp.dma_start(stage[:, c % RING], w_cols[:, c * CHUNK:(c + 1) * CHUNK]).then_inc(s_st[c % RING], 16)
                if c == STEPS:
                    load_x(0, 0)
            load_x(1, 1)
            sp.dma_start(acc[0:TOK, :], x.rearrange("b t d -> (b t) d")).then_inc(s_acc, 16)
            sp.wait_ge(s_padc, 3)
            sp.dma_start(acc[TOK:TOK + P, :], pad[:, 0:H]).then_inc(s_acc, 16)
            for n in range(WINDOW):
                a = E * REGION + n * P
                sp.dma_start(rows_dram[a:a + P, :], pad[:]).then_inc(s_acc, 16)
            sp.wait_ge(s_acc, 16 * (2 + WINDOW))
            load_x(2, 0)
            load_x(3, 1)
            load_tile_a(3)
            with sp.Fori(FIRST // 2, PAIRS - 1) as pr:
                for i in range(2):
                    load_tile(2 * (pr * 2 + i - FIRST) + 1)
                    load_x(pr * 2 + i, i)
                    load_tile_a(pr * 2 + i)
            for i in range(2):
                load_tile(2 * (NBLK - 2 + i - FIRST) + 1)
                load_tile_a(NBLK - 2 + i)
            load_tile(FQ + 1)
            sp.wait_ge(s_up, UP * (NBLK - UP_FROM) + 2)
            for e in range(E):
                n = sp.value_load(counts_i[0:1, e:e + 1], min_val=0, max_val=TOK)
                sp.dma_start(rows_dram[bass.ds(n + e * REGION, P), :], pad[:]).then_inc(s_fill, 16)
            sp.wait_ge(s_fill, 16 * E)
            sp.wait_ge(s_sc, 32 * NBLK)
            sp.wait_ge(s_up, UP * (NBLK - UP_FROM + 1) + 1)
            m = tiles_left(sp)
            with sp.Fori(FQ + 2, m + LEAST) as q:
                load_tile(q)
            sp.wait_ge(s_scat_last, 16)
            sp.dma_start(out.rearrange("b t d -> (b t) d"), acc[0:TOK, :]).then_inc(s_out, 16)
            sp.wait_ge(s_out, 16)

        @block.tensor
        def _(pe):
            def xw_mm(i, p, q, start=False):
                m, k = q // 3, q % 3
                dst = xw[p][:, i * P:(i + 1) * P].rearrange("p (t c b) -> p t c b", c=2, b=B)[:, :, m, :]
                flags = dict(start=start, stop=False, skip_group_check=True)
                if k == 0:
                    return pe.matmul(dst, b_sb[0:1, m * P:(m + 1) * P], ones[0:1, :], **flags)
                mv = xt[:, i, k - 1, :].rearrange("p (t a b) -> p t a b", a=2, b=B)[:, :, p, :]
                return pe.matmul(dst, wx_sb[:, k - 1, m * P:(m + 1) * P], mv, **flags)

            def next_xw(blk, i, tt):
                for p in range(2):
                    if tt in XW_AT[p]:
                        q = XW_AT[p].index(tt)
                        if tt == min(XW_AT[0] + XW_AT[1]):
                            pe.wait_ge(s_x[1 - i], 16 * ((blk + 1) // 2 + 1) if isinstance(blk, int) else
                                       (blk - i) * 8 + 16 * (1 + i))
                        mm = xw_mm(1 - i, p, q)
                        if tt == max(XW_AT[0] + XW_AT[1]):
                            mm.then_inc(s_xw, 1)

            def route(i, gi, tt):
                if tt == 1:
                    n = 0
                    for k in range(2):
                        for hp, gp in ((hi, gate_hi), (hi, gate_lo), (lo, gate_hi)):
                            mm = pe.matmul(p_lg, hp[:, i, k, :], gp[:, k, :], start=(n == 0), stop=(n == 5))
                            n += 1
                    mm.then_inc(s_lg, 1)
                if tt in (4, 6):
                    pe.wait_ge(s_rt, gi * RT + 1)
                    src = hi if tt == 4 else lo
                    for k in range(2):
                        c = (0 if tt == 4 else H) + k * P
                        mm = pe.transpose(p_rows[:, c:c + P], src[:, i, k, :], ident16[:])
                    mm.then_inc(s_tr, 1)
                if tt == 14:
                    pe.wait_ge(s_rows, gi * 4 + 4)
                    pe.wait_ge(s_rt, gi * RT + 13)
                    pe.matmul(p_rank, tri[:], chosen[:], start=True, stop=False)
                    pe.matmul(p_rank, all1[:], seen[:, i, :], start=False, stop=True)
                    pe.matmul(p_cnt, all1[:], seen[:, 1 - i, :], start=False, stop=True,
                              skip_group_check=True).then_inc(s_rk, 1)

            def turn_x(q):
                pe.wait_ge(s_xrow, 16 * (q + 1))
                for c in range(2 * KC):
                    mm = pe.transpose(p_x[:, c * P:(c + 1) * P], xrow16[:, c * P:(c + 1) * P], ident16[:])
                mm.then_inc(s_xtp, 1)

            def gate_up(e, up, h, banks, n0, n1):
                prods = [(xpart, w, k) for k in range(KC) for xpart, w in ((k, w_hi), (KC + k, w_hi), (k, w_lo))]
                dst = banks["u" if up else "g"][h]
                for n in range(n0, n1):
                    xpart, w, k = prods[n]
                    a = k * 2 * INNER + up * INNER + h * HALF
                    rhs = w[:, bass.ds(e, 1), a:a + HALF].rearrange("p a c -> p (a c)")
                    mm = pe.matmul(dst[:], x_T[:, xpart, :], rhs, start=(n == 0), stop=(n == 3 * KC - 1),
                                   skip_group_check=True)
                if n1 == 3 * KC:
                    mm.then_inc(s_u if up else s_g, 1)

            def turn_hidden(q, h, banks):
                pe.wait_ge(s_hid, 2 * q + h + 2)
                if h and banks is BETWEEN:
                    pe.wait_ge(s_hlo, 2 * q + 1)
                for c in range(HC):
                    a = h * HALF + c * P
                    mm = pe.transpose(banks["h"][h][:, c * P:(c + 1) * P], hid[:, a:a + P], ident32[:])
                mm.then_inc(s_th, 1)

            def down(e, q, n0, n1):
                if n0 == 0:
                    pe.wait_ge(s_hlo, 2 * q + 2)
                parts = ((hT_hi, w_hi), (hT_hi, w_lo), (hT_lo, w_hi))
                for n in range(n0, n1):
                    c, (hp, w) = n // 3, parts[n % 3]
                    rhs = w[:, bass.ds(e, 1), GU + c * H:GU + (c + 1) * H].rearrange("p a c -> p (a c)")
                    mm = pe.matmul(p_y[:, 0:H], hp[:, c, :], rhs, start=(n == 0), stop=(n == 3 * IC - 1))
                if n1 == 3 * IC:
                    mm.then_inc(s_d, 1)

            experts = {}

            def tile(blk, a, tt):
                q = 2 * (blk - FIRST) + a
                for h in range(2):
                    for up, at in ((0, G_AT[h]), (1, U_AT[h])):
                        if at <= tt < at + 3:
                            if tt == at:
                                if h == 0 and not up:
                                    pe.wait_ge(s_xt, q + 1)
                                    experts[a] = entry(pe, 0, q)
                                pe.wait_ge(s_hid if up else s_sil, 2 * q + h + 1)
                            gate_up(experts[a], up, h, BETWEEN, 2 * (tt - at), 2 * (tt - at) + 2)
                    if tt == TURN_AT[h]:
                        turn_hidden(q, h, BETWEEN)
                if DOWN_AT <= tt < DOWN_AT + 6:
                    down(experts[a], q, 4 * (tt - DOWN_AT), 4 * (tt - DOWN_AT) + 4)

            def step(blk, i, tt, routes, tiles, ahead, last):
                t = i * STEPS + tt
                n = blk * STEPS + tt
                pi, pt = (i, tt - 1) if tt else (1 - i, STEPS - 1)
                if tt in (2, 3):
                    pe.wait_ge(s_clr, 2 * blk + tt - 1)
                pe.wait_ge(s_hi, n + 1)
                for w in (wh_hi, wh_lo):
                    for m in range(2):
                        for k in range(2):
                            pe.matmul(preact(i, tt)[:, B * m:B * m + B], w[:, k, m * P:(m + 1) * P],
                                      hi[:, pi, k, B * pt:B * pt + B], start=False, stop=False, skip_group_check=True)
                pe.wait_ge(s_lo, n + 1)
                for m in range(2):
                    for k in range(2):
                        mm = pe.matmul(preact(i, tt)[:, B * m:B * m + B], wh_hi[:, k, m * P:(m + 1) * P],
                                       lo[:, pi, k, B * pt:B * pt + B], start=False, stop=False, skip_group_check=True)
                mm.then_inc(s_pre, 1)
                if not last:
                    next_xw(blk, i, tt)
                if routes:
                    if tt == 1 and tiles:
                        pe.wait_ge(s_xt, 2 * (blk - FIRST) + 1)
                    route(1 - i, blk - 1, tt)
                if tiles:
                    tile(blk, 0, tt)
                    tile(blk, 1, tt - TILE_B)
                    if tt == TURN_X_AT[1]:
                        pe.wait_ge(s_up, UP * (blk - UP_FROM) + 1)
                        turn_x(2 * (blk - FIRST) + 1)
                if ahead and tt == TURN_X_AT[0]:
                    if not tiles:
                        pe.wait_ge(s_up, UP * (blk - UP_FROM) + 1)
                    turn_x(2 * (blk + 1 - FIRST))

            def pair(pr):
                for i in range(2):
                    for tt in range(STEPS):
                        step(pr * 2 + i, i, tt, **modes(pr, i))

            pe.wait_ge(s_prep, 6)
            pe.wait_ge(s_c, 3)
            pe.wait_ge(s_cp, 5)
            pe.wait_ge(s_x[0], 16)
            for p in range(2):
                for q in range(6):
                    mm = xw_mm(0, p, q, start=(q == 0))
            mm.then_inc(s_xw, 1)
            pair(0)
            pair(1)
            with pe.Fori(FIRST // 2, PAIRS - 1) as pr:
                pair(pr)
            pair(PAIRS - 1)

            def all_gate_up(q):
                e = entry(pe, 0, q)
                pe.wait_ge(s_xt, q + 1)
                pe.wait_ge(s_hid, 2 * q + 1)
                for h in range(2):
                    for up in range(2):
                        gate_up(e, up, h, AFTER, 0, 3 * KC)

            def all_down(q):
                down(entry(pe, 0, q), q, 0, 3 * IC)

            def all_turn(q):
                for h in range(2):
                    turn_hidden(q, h, AFTER)

            pe.wait_ge(s_hi, T + 1)
            pe.wait_ge(s_lo, T + 1)
            pe.wait_ge(s_xt, FQ + 1)
            for tt in (1, 4, 6):
                route(1, NBLK - 1, tt)
            all_gate_up(FQ)
            route(1, NBLK - 1, 14)
            all_turn(FQ)
            pe.wait_ge(s_up, UP * (NBLK - UP_FROM) + 1)
            turn_x(FQ + 1)
            all_down(FQ)
            all_gate_up(FQ + 1)
            m = tiles_last(pe)
            turn_x(FQ + 2)
            all_turn(FQ + 1)
            with pe.Fori(FQ + 2, m + LEAST - 1) as q:
                all_gate_up(q)
                turn_x(q + 1)
                all_down(q - 1)
                all_turn(q)
            all_gate_up(m + LEAST - 1)
            all_down(m + LEAST - 2)
            all_turn(m + LEAST - 1)
            all_down(m + LEAST - 1)

        @block.scalar
        def _(act):
            def route(gi, tt):
                if 7 <= tt < 11:
                    n = tt - 7
                    act.wait_ge(s_tr, gi * 2 + 2)
                    if n == 0 and not is0(gi):
                        act.wait_ge(s_sc, gi * 32)
                    cols = slice((n % 2) * H, (n % 2 + 1) * H)
                    act.copy(rows16[:, n // 2, cols], p_rows[:, cols]).then_inc(s_rows, 1)
                if tt == 12:
                    act.wait_ge(s_rt, gi * RT + 10)
                    act.activation(st[:, 6:7], st[:, 5:6], ACT.Tanh, scale=0.5 / SCALE).then_inc(s_tanh, 1)

            def x_out(q):
                act.wait_ge(s_xtp, q + 1)
                act.copy(x_T[:].rearrange("p c t -> p (c t)"), p_x[:, 0:ROW]).then_inc(s_xt, 1)

            def silu(q, h, banks):
                act.wait_ge(s_g, 2 * q + 1 + h)
                act.activation(hid[:, h * HALF:(h + 1) * HALF], banks["g"][h][:], ACT.Silu,
                               scale=1 / SCALE).then_inc(s_sil, 1)

            def hidden_hi(q, h, banks):
                act.wait_ge(s_th, 2 * q + 1 + h)
                act.copy(hT_hi[:, h * HC:(h + 1) * HC, :].rearrange("p c t -> p (c t)"),
                         banks["h"][h][:]).then_inc(s_hhi, 1)

            def weigh(q):
                act.wait_ge(s_d, q + 1)
                act.wait_ge(s_mt, 3 * q + 3)
                act.activation(y_sb[:], p_y[:, 0:H], ACT.Copy, scale=weight_now[:, 0:1]).then_inc(s_y, 1)

            def tile(blk, a, tt):
                q = 2 * (blk - FIRST) + a
                for h in range(2):
                    if tt == SILU_AT[h]:
                        silu(q, h, BETWEEN)
                    if tt == HI_AT[h]:
                        hidden_hi(q, h, BETWEEN)
                if tt == Y_AT:
                    weigh(q)

            def split(c):
                act.wait_ge(s_st[c % RING], 16 * (c // RING + 1))
                act.activation(w_hi_cols[:, c * CHUNK:(c + 1) * CHUNK], stage[:, c % RING], ACT.Copy,
                               scale=SCALE).then_inc(s_ch, 1)

            def step(blk, i, tt, routes, tiles, ahead, last):
                n = blk * STEPS + tt
                act.wait_ge(s_pre, n + 1)
                src = preact(i, tt).rearrange("p (c b) -> p c b", c=2)
                act.activation(hi[:, i, :, B * tt:B * tt + B], src, ACT.Tanh, scale=1 / SCALE).then_inc(s_hi, 1)
                act.activation(h32[:, 4 * (tt % 2):4 * (tt % 2) + 4], preact(i, tt), ACT.Tanh,
                               scale=1 / SCALE).then_inc(s_h32, 1)
                if routes:
                    route(blk - 1, tt)
                if tiles:
                    tile(blk, 0, tt)
                    tile(blk, 1, tt - TILE_B)
                    if tt == X_OUT_AT[1]:
                        x_out(2 * (blk - FIRST) + 1)
                if ahead and tt == X_OUT_AT[0]:
                    x_out(2 * (blk + 1 - FIRST))
                if isinstance(blk, int) and blk < 2:
                    c = chunk_of(n)
                    if c is not None:
                        split(c)

            def pair(pr):
                for i in range(2):
                    for tt in range(STEPS):
                        step(pr * 2 + i, i, tt, **modes(pr, i))

            act.wait_ge(s_w, 96)
            act.activation(st[:, 7:8], h0[:, 0, 0:1], ACT.Silu).then_inc(s_sil, 1)
            act.copy(hi[:, 1, :, P - B:P], h0[:]).then_inc(s_hi, 1)
            pair(0)
            pair(1)
            with act.Fori(FIRST // 2, PAIRS - 1) as pr:
                pair(pr)
            pair(PAIRS - 1)

            for tt in range(7, 11):
                route(NBLK - 1, tt)
            route(NBLK - 1, 12)
            for h in range(2):
                silu(FQ, h, AFTER)
            for h in range(2):
                hidden_hi(FQ, h, AFTER)
            x_out(FQ + 1)
            weigh(FQ)
            for h in range(2):
                silu(FQ + 1, h, AFTER)
            m = tiles_last(act)
            x_out(FQ + 2)
            for h in range(2):
                hidden_hi(FQ + 1, h, AFTER)
            with act.Fori(FQ + 2, m + LEAST - 1) as q:
                silu(q, 0, AFTER)
                silu(q, 1, AFTER)
                x_out(q + 1)
                weigh(q - 1)
                hidden_hi(q, 0, AFTER)
                hidden_hi(q, 1, AFTER)
            silu(m + LEAST - 1, 0, AFTER)
            silu(m + LEAST - 1, 1, AFTER)
            weigh(m + LEAST - 2)
            hidden_hi(m + LEAST - 1, 0, AFTER)
            hidden_hi(m + LEAST - 1, 1, AFTER)
            weigh(m + LEAST - 1)

        @block.vector
        def _(v):
            def route(i, gi, tt):
                def done(k):
                    v.wait_ge(s_rt, gi * RT + k)

                def op(o):
                    o.then_inc(s_rt, 1)

                if tt == 2:
                    v.wait_ge(s_lg, gi + 1)
                    op(v.tensor_copy(lg[:], p_lg))
                if tt == 3:
                    done(1)
                    op(v.tensor_reduce(st[:, 0:1], lg[:], AX.X, ALU.max))
                if tt == 4:
                    done(2)
                    op(v.scalar_tensor_tensor(out=pick[:], in0=lg[:], scalar=st[:, 0:1], in1=rev[:],
                                              op0=ALU.is_equal, op1=ALU.mult))
                if tt == 5:
                    done(3)
                    op(v.tensor_reduce(st[:, 4:5], pick[:], AX.X, ALU.max))
                if tt == 6:
                    done(4)
                    op(v.tensor_scalar(oh1[:], rev[:], st[:, 4:5], None, ALU.is_equal))
                if tt == 7:
                    done(5)
                    op(v.scalar_tensor_tensor(out=lg2[:], in0=oh1[:], scalar=NEG, in1=lg[:],
                                              op0=ALU.mult, op1=ALU.add))
                if tt == 8:
                    done(6)
                    op(v.tensor_reduce(st[:, 1:2], lg2[:], AX.X, ALU.max))
                if tt == 9:
                    done(7)
                    op(v.scalar_tensor_tensor(out=pick[:], in0=lg2[:], scalar=st[:, 1:2], in1=rev[:],
                                              op0=ALU.is_equal, op1=ALU.mult))
                if tt == 10:
                    done(8)
                    op(v.tensor_reduce(st[:, 4:5], pick[:], AX.X, ALU.max))
                    op(v.tensor_tensor(st[:, 5:6], st[:, 0:1], st[:, 1:2], ALU.subtract))
                if tt == 11:
                    done(10)
                    op(v.tensor_scalar(oh2[:], rev[:], st[:, 4:5], None, ALU.is_equal))
                if tt == 12:
                    done(11)
                    op(v.tensor_tensor(chosen[:], oh1[:], oh2[:], ALU.add))
                if tt == 13:
                    done(12)
                    op(v.tensor_tensor(seen[:, 1 - i, :], seen[:, i, :], chosen[:], ALU.add))
                if tt == 15:
                    v.wait_ge(s_rk, gi + 1)
                    done(13)
                    op(v.tensor_tensor(rank[:], p_rank, base[:], ALU.add))
                if tt == 16:
                    done(14)
                    op(v.tensor_tensor_reduce(pick[:], oh1[:], rank[:], 1.0, 0.0, ALU.mult, ALU.add, st[:, 2:3]))
                if tt == 17:
                    done(15)
                    op(v.tensor_tensor_reduce(pick[:], oh2[:], rank[:], 1.0, 0.0, ALU.mult, ALU.add, st[:, 3:4]))
                    v.wait_ge(s_tanh, gi + 1)
                    if not is0(gi):
                        v.wait_ge(s_sc, gi * 32)
                    op(v.tensor_scalar(meta[:, 0, 1:2], st[:, 6:7], 0.5 / SCALE, 0.5 / SCALE, ALU.mult, ALU.add))
                if tt == 18:
                    op(v.tensor_scalar(meta[:, 1, 1:2], st[:, 6:7], -0.5 / SCALE, 0.5 / SCALE, ALU.mult, ALU.add))
                    op(v.tensor_copy(meta[:, :, 0:1], tok[:].unsqueeze(1).to_broadcast([P, 2, 1])))
                if tt == 19:
                    done(19)
                    op(v.tensor_scalar(tok[:], tok[:], float(STEPS), None, ALU.add))
                    v.wait_ge(s_rows, gi * 4 + 4)
                    op(v.tensor_copy(slot[:], st[:, 2:4]))

            def update(n, k, flush=False):
                if k == 15:
                    regs["at"] = v.value_load(qi, min_val=0, max_val=QMAX)
                if k:
                    v.wait_ge(s_up, UP * n + k + (1 if flush else 0))
                j3 = cmp[:, 0:WINDOW * E].rearrange("p (j e) -> p j e", e=E)
                q3 = cmp[:, 0:E * NBLK].rearrange("p (e q) -> p e q", e=E)
                e3 = cmp[:, 0:E * E].rearrange("p (e q) -> p e q", e=E)

                def each(a):
                    return a.unsqueeze(1).to_broadcast([1, WINDOW, E])

                if k == 0:
                    o = v.tensor_copy(cnt, p_cnt[0:1, :])
                elif k == 1:
                    o = v.tensor_tensor(q3, cnt.unsqueeze(2).to_broadcast([1, E, NBLK]),
                                        (frow if flush else qrow).unsqueeze(1).to_broadcast([1, E, NBLK]), ALU.is_ge)
                elif k == 2:
                    o = v.tensor_reduce(full, q3, AX.X, ALU.add)
                elif k == 3:
                    o = v.tensor_tensor(new, full, had[:, 0:E], ALU.subtract)
                elif k == 4:
                    o = v.tensor_tensor(e3, tri8, new.unsqueeze(1).to_broadcast([1, E, E]), ALU.mult)
                elif k == 5:
                    o = v.tensor_reduce(upto, e3, AX.X, ALU.add)
                elif k == 6:
                    o = v.tensor_tensor(j3, irow.unsqueeze(2).to_broadcast([1, WINDOW, E]), each(upto), ALU.is_ge)
                elif k == 7:
                    o = v.tensor_reduce(ej, j3, AX.X, ALU.add)
                elif k == 8:
                    o = v.tensor_tensor(step_e, had[:, 1:E + 1], had[:, 0:E], ALU.subtract)
                elif k == 9:
                    o = v.tensor_tensor(step_e, step_e, new, ALU.subtract)
                elif k == 10:
                    o = v.tensor_tensor(j3, j3, each(step_e), ALU.mult)
                elif k == 11:
                    o = v.tensor_reduce(sj, j3, AX.X, ALU.add)
                elif k == 12:
                    o = v.tensor_tensor(sj, sj, irow, ALU.add)
                elif k == 13:
                    o = v.tensor_scalar(sj, sj, had[:, 0:1], float(P), ALU.add, ALU.mult)
                elif k == 14:
                    o = v.scalar_tensor_tensor(out=gj, in0=ej, scalar=float(REGION), in1=sj,
                                               op0=ALU.mult, op1=ALU.add)
                elif k == 15:
                    o = v.tensor_scalar(queue[0:1, 0, bass.ds(regs["at"], WINDOW)], ej, float(E - 1), None, ALU.min)
                elif k == 16:
                    o = v.tensor_copy(queue[0:1, 1, bass.ds(regs["at"], WINDOW)], gj)
                elif k == 17:
                    o = v.tensor_copy(had[:, 0:E], full)
                elif k == 18:
                    o = v.tensor_scalar(floor, floor, 2.0, None, ALU.add)
                elif k == 19:
                    o = v.scalar_tensor_tensor(out=place, in0=upto[:, E - 1:E], scalar=place, in1=floor,
                                               op0=ALU.add, op1=ALU.max)
                elif k == 20:
                    o = v.tensor_copy(qi, place)
                else:
                    o = v.tensor_scalar(left, place, -float(LEAST), 0.0, ALU.add, ALU.max)
                o.then_inc(s_up, 1)

            regs = {}

            def times_up(q, h, banks):
                v.wait_ge(s_sil, 2 * q + 2 + h)
                v.wait_ge(s_u, 2 * q + 1 + h)
                part = hid[:, h * HALF:(h + 1) * HALF]
                v.scalar_tensor_tensor(out=part, in0=banks["u"][h][:], scalar=1 / SCALE, in1=part,
                                       op0=ALU.mult, op1=ALU.mult).then_inc(s_hid, 1)

            def hidden_lo(q, h, banks):
                v.wait_ge(s_hhi, 2 * q + 1 + h)
                cs = slice(h * HC, (h + 1) * HC)
                v.tensor_tensor(hT_lo[:, cs, :].rearrange("p c t -> p (c t)"), banks["h"][h][:],
                                hT_hi[:, cs, :].rearrange("p c t -> p (c t)"), ALU.subtract).then_inc(s_hlo, 1)

            def take(q):
                v.wait_ge(s_xrow, 16 * (q + 1))
                if not is0(q):
                    v.wait_ge(s_mt, 3 * q)
                v.tensor_copy(meta_in[:], xrow_meta).then_inc(s_mt, 1)

            def shift(q):
                v.wait_ge(s_mt, 3 * q + 1)
                if not is0(q):
                    v.wait_ge(s_scat, 16 * q)
                v.tensor_copy(place_now[:], meta_in[:, 0:1]).then_inc(s_mt, 1)
                v.tensor_copy(weight_now[:], meta_in[:, 1:2]).then_inc(s_mt, 1)

            def tile(blk, a, tt):
                q = 2 * (blk - FIRST) + a
                for h in range(2):
                    if tt == MUL_AT[h]:
                        times_up(q, h, BETWEEN)
                    if tt == LO_AT[h]:
                        hidden_lo(q, h, BETWEEN)

            def split(c):
                v.wait_ge(s_ch, c + 1)
                cols = slice(c * CHUNK, (c + 1) * CHUNK)
                v.scalar_tensor_tensor(out=w_lo_cols[:, cols], in0=stage[:, c % RING], scalar=SCALE,
                                       in1=w_hi_cols[:, cols], op0=ALU.mult, op1=ALU.subtract).then_inc(s_cl, 1)

            def step(blk, i, tt, routes, tiles, ahead, last):
                n = blk * STEPS + tt
                v.wait_ge(s_h32, n + 1)
                v.tensor_tensor(lo[:, i, :, B * tt:B * tt + B],
                                h32[:, 4 * (tt % 2):4 * (tt % 2) + 4].rearrange("p (c b) -> p c b", c=2),
                                hi[:, i, :, B * tt:B * tt + B], ALU.subtract).then_inc(s_lo, 1)
                if tt < 2:
                    v.memset(xw[tt % 2][:, (1 - i) * P:(2 - i) * P], 0.0).then_inc(s_clr, 1)
                if routes:
                    route(1 - i, blk - 1, tt)
                    if not isinstance(blk, int) or blk >= UP_FROM:
                        if tt == 16:
                            update(blk - UP_FROM, 0)
                        if tt in UPDATE_AT[1:]:
                            update(blk - UP_FROM, UPDATE_AT.index(tt))
                if tiles:
                    tile(blk, 0, tt)
                    tile(blk, 1, tt - TILE_B)
                    if tt == TAKE_AT[1]:
                        take(2 * (blk - FIRST) + 1)
                    if tt == SHIFT_AT[1]:
                        shift(2 * (blk - FIRST) + 1)
                if ahead:
                    if tt == TAKE_AT[0]:
                        take(2 * (blk + 1 - FIRST))
                    if tt == SHIFT_AT[0]:
                        shift(2 * (blk + 1 - FIRST))
                if isinstance(blk, int) and blk < 2:
                    c = chunk_of(n)
                    if c is not None:
                        split(c)

            def pair(pr):
                for i in range(2):
                    for tt in range(STEPS):
                        step(pr * 2 + i, i, tt, **modes(pr, i))

            v.memset(ones[:], 1.0).then_inc(s_c, 1)
            v.memset(all1[:], 1.0).then_inc(s_c, 1)
            v.memset(seen[:], 0.0).then_inc(s_c, 1)
            v.memset(rows[:, :, H:], 0.0)
            v.memset(had, 0.0)
            v.memset(place, 0.0)
            v.memset(qi.bitcast(F32), 0.0)
            v.memset(floor, -2.0).then_inc(s_hid, 1)
            v.wait_ge(s_w, 96)
            v.tensor_scalar(wh_hi[:], wh_sb, SCALE, None, ALU.mult).then_inc(s_prep, 1)
            v.tensor_scalar(gate_hi[:], gate_sb, SCALE, None, ALU.mult).then_inc(s_prep, 1)
            v.tensor_scalar(wx_sb[:], wx_sb[:], SCALE, None, ALU.mult).then_inc(s_prep, 1)
            v.tensor_scalar(b_sb[:], b_sb[:], SCALE, None, ALU.mult).then_inc(s_prep, 1)
            v.wait_ge(s_prep, 4)
            v.scalar_tensor_tensor(out=wh_lo[:], in0=wh_sb, scalar=SCALE, in1=wh_hi[:],
                                   op0=ALU.mult, op1=ALU.subtract).then_inc(s_prep, 1)
            v.scalar_tensor_tensor(out=gate_lo[:], in0=gate_sb, scalar=SCALE, in1=gate_hi[:],
                                   op0=ALU.mult, op1=ALU.subtract).then_inc(s_prep, 1)
            v.wait_ge(s_hi, 1)
            v.tensor_tensor(lo[:, 1, :, P - B:P], h0[:], hi[:, 1, :, P - B:P], ALU.subtract).then_inc(s_lo, 1)
            v.wait_ge(s_cp, 5)
            v.wait_ge(s_padc, 3)
            v.wait_ge(s_hid, 1)
            pair(0)
            pair(1)
            with v.Fori(FIRST // 2, PAIRS - 1) as pr:
                pair(pr)
            pair(PAIRS - 1)

            for tt in range(2, 14):
                route(1, NBLK - 1, tt)
            for h in range(2):
                times_up(FQ, h, AFTER)
            for tt in range(15, 20):
                route(1, NBLK - 1, tt)
            last = NBLK - UP_FROM
            update(last, 0)
            v.wait_ge(s_up, UP * last + 1)
            v.tensor_copy(counts_i[:], cnt).then_inc(s_up, 1)
            take(FQ + 1)
            for h in range(2):
                hidden_lo(FQ, h, AFTER)
            for k in range(1, UP):
                update(last, k, flush=True)
            shift(FQ + 1)
            for h in range(2):
                times_up(FQ + 1, h, AFTER)
            m = tiles_last(v)
            take(FQ + 2)
            for h in range(2):
                hidden_lo(FQ + 1, h, AFTER)
            with v.Fori(FQ + 2, m + LEAST - 1) as q:
                times_up(q, 0, AFTER)
                times_up(q, 1, AFTER)
                shift(q)
                take(q + 1)
                hidden_lo(q, 0, AFTER)
                hidden_lo(q, 1, AFTER)
            times_up(m + LEAST - 1, 0, AFTER)
            times_up(m + LEAST - 1, 1, AFTER)
            shift(m + LEAST - 1)
            hidden_lo(m + LEAST - 1, 0, AFTER)
            hidden_lo(m + LEAST - 1, 1, AFTER)

        @block.gpsimd
        def _(pool):
            def iota(out, pattern, base_, mult=0):
                return pool.iota(out, pattern, base=base_, channel_multiplier=mult,
                                 allow_small_or_imprecise_dtypes=True)

            pool.memset(ident32[:], 0.0).then_inc(s_cp, 1)
            pool.memset(tri[:], 1.0).then_inc(s_cp, 1)
            pool.memset(tri8, 1.0).then_inc(s_padc, 1)
            pool.memset(pad[:], 0.0).then_inc(s_padc, 1)
            pool.wait_ge(s_cp, 2)
            pool.affine_select(out=ident32[:], in_=ident32[:], compare_op=ALU.not_equal, fill=1.0, base=0,
                               pattern=[[-1, P]], channel_multiplier=1).then_inc(s_cp, 1)
            pool.affine_select(out=tri[:], in_=tri[:], compare_op=ALU.is_gt, fill=0.0, base=0,
                               pattern=[[1, P]], channel_multiplier=-1)
            iota(rev[:], [[-1, E]], E)
            iota(base[:], [[REGION, E]], 0).then_inc(s_cp, 1)
            pool.wait_ge(s_cp, 4)
            pool.tensor_copy(ident16[:], ident32[:]).then_inc(s_cp, 1)
            pool.wait_ge(s_padc, 2)
            pool.affine_select(out=tri8, in_=tri8, compare_op=ALU.is_ge, fill=0.0, base=0,
                               pattern=[[1, E], [-1, E]], channel_multiplier=0)
            iota(irow, [[1, WINDOW]], 0)
            iota(qrow, [[P, NBLK]], P)
            iota(frow, [[P, NBLK]], 1)
            iota(pad[:, H:H + 1], [[0, 1]], TOK, 1).then_inc(s_padc, 1)

            routed = pool.alloc_register("routed_count")
            ready = pool.alloc_register("ready_count")
            pool.reg_mov(routed, RT)
            pool.reg_mov(ready, 1)

            def scatter_rows():
                pool.wait_ge(s_cp, 5)
                pool.wait_ge(s_rt, routed)
                for k in range(2):
                    pool.indirect_dma_start(rows_dram, bass.IndirectOffsetOnAxis(ap=slot[:, k:k + 1], axis=0),
                                            rows[:, k, :], None).then_inc(s_sc, 16)
                pool.reg_add(routed, routed, RT)

            def add_results(s=s_scat):
                pool.wait_ge(s_acc, 16 * (2 + WINDOW))
                pool.wait_ge(s_y, ready)
                pool.indirect_dma_start(acc, bass.IndirectOffsetOnAxis(ap=place_now[:, 0:1], axis=0),
                                        y_sb[:], None, compute_op=ALU.add).then_inc(s, 16)
                pool.reg_add(ready, ready, 1)

            for _ in range(FIRST - 1):
                scatter_rows()
            with pool.Fori(FIRST, NBLK):
                scatter_rows()
                add_results()
                add_results()
            scatter_rows()
            add_results()
            add_results()
            m = tiles_last(pool)
            with pool.Fori(FQ + 2, m + LEAST - 1):
                add_results()
            add_results(s_scat_last)


def kernel(x, cond_1024, L0_cond_Wx, L0_cond_Wh, L0_cond_b, L0_ffn_gate_w, L0_ffn_wg, L0_ffn_wu, L0_ffn_wd):
    import concourse.bacc as bacc
    import numpy as np
    from concourse.bass_utils import run_bass_kernel_spmd

    a = np.asarray
    x = a(x)
    b, t, d = x.shape
    e, inner, _ = L0_ffn_wg.shape
    kc = d // P

    def chunks(m):
        return np.ascontiguousarray(m.reshape(kc, P, *m.shape[1:]).swapaxes(0, 1))

    wg = a(L0_ffn_wg).transpose(2, 0, 1).reshape(kc, P, e, 1, inner)
    wu = a(L0_ffn_wu).transpose(2, 0, 1).reshape(kc, P, e, 1, inner)
    gu = np.concatenate([wg, wu], axis=3).transpose(1, 2, 0, 3, 4).reshape(P, e, -1)
    dn = a(L0_ffn_wd).transpose(2, 0, 1).reshape(inner // P, P, e, d).transpose(1, 2, 0, 3).reshape(P, e, -1)
    arrays = {
        "xT": chunks(x.transpose(2, 1, 0).reshape(d, t * b)),
        "x_in": np.ascontiguousarray(x),
        "h0T": chunks(a(cond_1024).T),
        "wx_in": np.ascontiguousarray(a(L0_cond_Wx)),
        "wh_in": np.ascontiguousarray(a(L0_cond_Wh)),
        "bias_in": np.ascontiguousarray(a(L0_cond_b)).reshape(1, -1),
        "gateT": chunks(a(L0_ffn_gate_w).T),
        "w_all": np.ascontiguousarray(np.concatenate([gu, dn], axis=2)),
        "tok0": np.array([[(p % b) * t + p // b] for p in range(P)], np.float32),
    }
    nc = bacc.Bacc("TRN2", target_bir_lowering=False, num_devices=1, dynamic_dma_scratch_size=4096)
    args = [nc.dram_tensor(k, v.shape, mybir.dt.from_np(v.dtype), kind="ExternalInput").ap() for k, v in arrays.items()]
    out = nc.dram_tensor("out", x.shape, F32, kind="ExternalOutput").ap()
    build(nc, *args, out)
    result = run_bass_kernel_spmd(nc, [arrays], core_ids=[0])
    return result.results[0]["out"]
```

```python
from contextlib import ExitStack

import concourse.bass as bass
from concourse import mybir

F32 = mybir.dt.float32
F16 = mybir.dt.float16
I32 = mybir.dt.int32
ALU = mybir.AluOpType
ACT = mybir.ActivationFunctionType
AX = mybir.AxisListType

P = 128
SCALE = 16.0
NEG = -3.0e38
PAD = 8

ROWS_AT = (4, 5, 6, 9)
ROWS_TURN_AT = (2, 3)
ENTRY_AT = (1, 33)
TILE_AT = (4, 34)
G_AT, U_AT = (0, 6), (3, 9)
SILU_AT, MUL_AT = (3, 4, 9, 10), (6, 7, 12, 13)
TURN_AT = (12, 13, 18, 19)
HI_AT, LO_AT = (14, 15, 20, 21), (16, 17, 22, 23)
DOWN_AT = (20, 21, 22, 23, 25, 26, 27, 28)
SHIFT_AT, Y_AT = 14, 29
TURN_X_AT, X_OUT_AT = (58, 19), ((59, 60), (20, 21))
TAKE_AT = (58, 19)
XW_AT = ((19, 21, 23, 49, 51, 63), (18, 20, 22, 28, 48, 50))
UPDATE_AT = (26, 27, 28, 29, 30, 31, 32, 33, 34, 35, 36, 37, 39, 40, 41, 42, 43, 45, 47, 50, 51, 52)
FIRST = 4


def build(nc, xT, x, h0T, wx, wh, bias, gateT, w_all, tok0, out):
    B, T, D = x.shape
    H = wh.shape[0]
    E = gateT.shape[2]
    KC = H // P
    TOK = B * T
    STEPS = P // B
    NBLK = T // STEPS
    PAIRS = NBLK // 2
    WIN = 2 * STEPS
    WCOL = w_all.shape[2]
    INNER = WCOL // (3 * KC)
    HALF = INNER // 2
    IC = INNER // P
    HC = IC // 2
    QC = IC // 4 * P
    GU = KC * 2 * INNER
    CHUNK = 512
    NCH = E * WCOL // CHUNK
    RING = 4
    REGION = TOK + P
    ROW = 2 * H
    ROWP = H + PAD
    WINDOW = 2 * E
    FQ = 2 * (NBLK - FIRST)
    LEAST = FQ + 4
    QMAX = FQ + 2 * TOK // P + E - 1
    NQ = QMAX + 2 * WINDOW
    RT = 21
    UP = len(UPDATE_AT)
    UP_FROM = 2
    assert KC == 2 and B == 2 and HALF == 512 and 2 * NCH <= 3 * STEPS and FIRST % 2 == 0

    rows_dram = nc.dram_tensor("expert_rows", (E * REGION + WINDOW * P, ROWP), F32, kind="Internal").ap()
    w_cols = w_all.rearrange("p e c -> p (e c)")

    with ExitStack() as ctx:
        def sb(name, shape, dt):
            return ctx.enter_context(nc.sbuf_tensor(name, shape, dt))

        def ps(name, shape, dt):
            return ctx.enter_context(nc.psum_tensor(name, shape, dt))

        def sem(name):
            return ctx.enter_context(nc.semaphore(name))

        w_hi = sb("w_hi", [P, E, WCOL], F16)
        w_lo = sb("w_lo", [P, E, WCOL], F16)
        w_hi_cols = w_hi[:].rearrange("p e c -> p (e c)")
        w_lo_cols = w_lo[:].rearrange("p e c -> p (e c)")
        ident32 = sb("ident32", [P, P], F32)
        ident16 = sb("ident16", [P, P], F16)
        tri = sb("tri", [P, P], F16)
        all1 = sb("all1", [P, P], F16)

        wx_sb = sb("wx_sb", [P, 2, H], F32)
        wh_hi = sb("wh_hi", [P, 2, H], F16)
        wh_lo = sb("wh_lo", [P, 2, H], F16)
        wh_hi_cols = wh_hi[:].rearrange("p k n -> p (k n)")
        b_sb = sb("b_sb", [1, H], F32)
        ones = sb("ones", [1, STEPS], F32)
        h0 = sb("h0", [P, 2, B], F32)
        hi = sb("hi", [P, 2, 2, P], F16)
        lo = sb("lo", [P, 2, 2, P], F16)
        xt = sb("xt", [P, 2, 2, P], F32)

        gate_hi = sb("gate_hi", [P, 2, E], F16)
        gate_lo = sb("gate_lo", [P, 2, E], F16)
        rev = sb("rev", [P, E], F32)
        base = sb("base", [P, E], F32)
        seen = sb("seen", [P, 2, E], F16)
        lg = sb("lg", [P, E], F32)
        lg2 = sb("lg2", [P, E], F32)
        pick = sb("pick", [P, E], F32)
        oh1 = sb("oh1", [P, E], F32)
        oh2 = sb("oh2", [P, E], F32)
        chosen = sb("chosen", [P, E], F16)
        rank = sb("rank", [P, E], F32)
        st = sb("st", [P, 8], F32)
        slot = sb("slot", [P, 2], I32)
        tok = sb("tok", [P, 1], F32)
        rows = sb("rows", [P, 2, ROWP], F32)
        rows16 = rows[:, :, 0:H].bitcast(F16)
        meta = rows[:, :, H:H + 2]
        pad = sb("pad", [P, ROWP], F32)

        queue = sb("queue", [1, 2, NQ], I32)
        counts_i = sb("counts_i", [1, E], I32)
        small = sb("small", [1, 448], F32)
        cut, at = {}, 0
        for name, n in dict(cmp=P, cnt=E, full=E, new=E, upto=E, step=E, had=E + 1, place=1, floor=1, qi=1, left=1,
                            ej=WINDOW, sj=WINDOW, gj=WINDOW, irow=WINDOW, qrow=NBLK, frow=NBLK, tri8=E * E).items():
            cut[name] = small[0:1, at:at + n]
            at += n
        cmp, cnt, full, new, upto, step_e, had, place, floor, qi, left, ej, sj, gj, irow, qrow, frow, tri8 = cut.values()
        qi, left = qi.bitcast(I32), left.bitcast(I32)
        tri8 = tri8.rearrange("p (a b) -> p a b", a=E)

        xrow = sb("xrow", [P, ROWP], F32)
        xrow16 = xrow[:, 0:H].bitcast(F16)
        xrow_meta = xrow[:, H:H + 2]
        x_T = sb("x_T", [P, 2 * KC, P], F16)
        meta_in = sb("meta_in", [P, 2], F32)
        place_now = sb("place_now", [P, 1], I32)
        weight_now = sb("weight_now", [P, 1], F32)
        y_sb = sb("y_sb", [P, H], F32)
        arena = sb("arena", [P, 2 * INNER], F32)
        hid = arena[:, 0:INNER]
        hT_hi = arena[:, INNER:INNER + INNER // 2].bitcast(F16)
        hT_lo = arena[:, INNER + INNER // 2:2 * INNER].bitcast(F16)
        stage = arena[:].rearrange("p (a c) -> p a c", a=RING)
        wh_sb = stage[:, 0, :].rearrange("p (k n) -> p k n", k=2)
        gate_sb = stage[:, 1, 0:2 * E].rearrange("p (k e) -> p k e", k=2)

        bank = [ps(f"bank{n}", [P, 512], F32) for n in range(8)]
        xw = bank[0:2]
        h32 = bank[2]
        p_y = bank[6]
        misc = bank[7]
        p_x = misc[:, 0:ROW // 2].bitcast(F16)
        p_rows = p_x
        p_lg = misc[:, 0:E]
        p_rank = misc[:, 256:256 + E]
        p_cnt = misc[:, 320:320 + E]
        BETWEEN = dict(g=(bank[3], bank[3]), u=(bank[4], bank[4]), h=(bank[5], bank[5]))
        AFTER = dict(g=(bank[3], bank[0]), u=(bank[4], bank[1]), h=(bank[5], bank[2]))

        s_w = sem("weights_in")
        s_x = [sem("x_in0"), sem("x_in1")]
        s_st = [sem(f"stage_in{n}") for n in range(RING)]
        s_c = sem("consts_vector")
        s_cp = sem("consts_pool")
        s_padc = sem("pad_made")
        s_prep = sem("weights_split")
        s_xw = sem("xw_done")
        s_clr = sem("xw_cleared")
        s_pre = sem("preact")
        s_hi = sem("h_hi")
        s_h32 = sem("h_full")
        s_lo = sem("h_lo")
        s_lg = sem("logits")
        s_tr = sem("rows_turned")
        s_rows = sem("rows_copied")
        s_rt = sem("routed")
        s_tanh = sem("weight_tanh")
        s_rk = sem("ranks")
        s_sc = sem("rows_scattered")
        s_ch = sem("chunk_hi")
        s_cl = sem("chunk_lo")
        s_up = sem("queue_updated")
        s_cnt = sem("counts_before_last_block")
        s_fill = sem("padded")
        s_acc = sem("accumulator_started")
        s_xrow = sem("tile_in")
        s_xtp = sem("tile_turned")
        s_xt = sem("tile_T")
        s_g = sem("gate_done")
        s_u = sem("up_done")
        s_sil = sem("silu_done")
        s_hid = sem("hidden_done")
        s_th = sem("hidden_turned")
        s_hhi = sem("hT_hi_done")
        s_hlo = sem("hT_lo_done")
        s_d = sem("down_done")
        s_mt = sem("meta_moved")
        s_y = sem("y_ready")
        s_scat = sem("y_added")
        s_scat_last = sem("y_added_last")

        block = ctx.enter_context(nc.Block())

        def preact(i, t):
            c = i * P + (t // 2) * 4
            return xw[t % 2][:, c:c + 4]

        def is0(v):
            return isinstance(v, int) and v == 0

        def entry(eng, which, q):
            a = queue[0:1, which, q:q + 1] if isinstance(q, int) else queue[0:1, which, bass.ds(q, 1)]
            if which == 0:
                return nc.s_assert_within(eng.value_load(a), 0, E - 1, skip_runtime_bounds_check_because=(
                    "the queue's experts are counts of comparisons, and held at E - 1 when they are written"))
            return eng.value_load(a, min_val=0, max_val=E * REGION + (WINDOW - 1) * P)

        def tiles_left(eng):
            return eng.value_load(left, min_val=0, max_val=QMAX - LEAST)

        def split_of(blk, tt):
            n = blk * STEPS + tt - 4 if isinstance(blk, int) else -1
            return n if 0 <= n < 2 * NCH else None

        def half_stage(n):
            return stage[:, n // 2 % RING, (n % 2) * CHUNK // 2:(n % 2 + 1) * CHUNK // 2]

        def modes(pr, i):
            blk = pr * 2 + i if isinstance(pr, int) else None
            return dict(routes=blk != 0, tiles=blk is None or blk >= FIRST, ahead=blk is None or blk >= FIRST - 1,
                        last=blk == NBLK - 1)

        def tiles_last(eng):
            eng.wait_ge(s_up, UP * (NBLK - UP_FROM + 1))
            return tiles_left(eng)

        @block.sync
        def _(sp):
            sp.dma_start(wh_sb, wh.rearrange("(k p) n -> p k n", p=P)).then_inc(s_w, 16)
            sp.dma_start(wx_sb[:], wx.rearrange("(k p) n -> p k n", p=P)).then_inc(s_w, 16)
            sp.dma_start(b_sb[:], bias).then_inc(s_w, 16)
            sp.dma_start(h0[:], h0T).then_inc(s_w, 16)
            sp.dma_start(gate_sb, gateT).then_inc(s_w, 16)
            sp.dma_start(tok[:], tok0).then_inc(s_w, 16)
            for i in range(2):
                sp.dma_start(xt[:, i], xT[:, :, i * P:(i + 1) * P]).then_inc(s_x[i], 16)

            def load_x(blk, i):
                sp.wait_ge(s_xw, blk + 1)
                sp.dma_start(xt[:, i], xT[:, :, bass.ds((blk + 2) * P, P)]).then_inc(s_x[i], 16)

            def load_tile(q):
                if not is0(q):
                    sp.wait_ge(s_xtp, q)
                    sp.wait_ge(s_mt, 3 * q - 2)
                row = entry(sp, 1, q)
                sp.dma_start(xrow[:], rows_dram[bass.ds(row, P), :]).then_inc(s_xrow, 16)

            def load_tile_a(blk):
                sp.wait_ge(s_up, UP * (blk - UP_FROM + 1))
                sp.wait_ge(s_sc, scattered)
                sp.reg_add(scattered, scattered, 32)
                load_tile(2 * (blk + 1 - FIRST))

            scattered = sp.alloc_register("scattered_count")
            sp.reg_mov(scattered, 32 * (FIRST - 1))

            sp.wait_ge(s_prep, 6)
            for c in range(NCH):
                if c >= RING:
                    sp.wait_ge(s_cl, 2 * (c - RING + 1))
                sp.dma_start(stage[:, c % RING], w_cols[:, c * CHUNK:(c + 1) * CHUNK]).then_inc(s_st[c % RING], 16)
                if c in (16, 48, 80):
                    load_x((c - 16) // 32, (c - 16) // 32 % 2)
            sp.dma_start(out[0:TOK, :], x.rearrange("b t d -> (b t) d")).then_inc(s_acc, 16)
            sp.wait_ge(s_padc, 3)
            sp.dma_start(out[TOK:TOK + P, :], pad[:, 0:H]).then_inc(s_acc, 16)
            for n in range(WINDOW):
                a = E * REGION + n * P
                sp.dma_start(rows_dram[a:a + P, :], pad[:]).then_inc(s_acc, 16)
            sp.wait_ge(s_acc, 16 * (2 + WINDOW))
            load_x(3, 1)
            load_tile_a(3)
            with sp.Fori(FIRST // 2, PAIRS - 1) as pr:
                for i in range(2):
                    load_tile(2 * (pr * 2 + i - FIRST) + 1)
                    load_x(pr * 2 + i, i)
                    load_tile_a(pr * 2 + i)
            for i in range(2):
                load_tile(2 * (NBLK - 2 + i - FIRST) + 1)
                if i == 1:
                    sp.wait_ge(s_cnt, 1)
                    sp.wait_ge(s_sc, 32 * (NBLK - 1))
                    for e in range(E):
                        n = sp.value_load(counts_i[0:1, e:e + 1], min_val=0, max_val=TOK - P)
                        for a in (0, P):
                            sp.dma_start(rows_dram[bass.ds(n + (e * REGION + a), P), :], pad[:]).then_inc(s_fill, 16)
                    sp.wait_ge(s_fill, 32 * E)
                load_tile_a(NBLK - 2 + i)
            load_tile(FQ + 1)
            sp.wait_ge(s_sc, 32 * NBLK)
            sp.wait_ge(s_up, UP * (NBLK - UP_FROM) + 17)
            load_tile(FQ + 2)
            m = tiles_last(sp)
            with sp.Fori(FQ + 3, m + LEAST) as q:
                load_tile(q)
            sp.wait_ge(s_scat_last, 16)

        @block.tensor
        def _(pe):
            def xw_mm(i, p, q, start=False):
                m, k = q // 3, q % 3
                dst = xw[p][:, i * P:(i + 1) * P].rearrange("p (t c b) -> p t c b", c=2, b=B)[:, :, m, :]
                flags = dict(start=start, stop=False, skip_group_check=True)
                if k == 0:
                    return pe.matmul(dst, b_sb[0:1, m * P:(m + 1) * P], ones[0:1, :], **flags)
                mv = xt[:, i, k - 1, :].rearrange("p (t a b) -> p t a b", a=2, b=B)[:, :, p, :]
                return pe.matmul(dst, wx_sb[:, k - 1, m * P:(m + 1) * P], mv, **flags)

            def next_xw(blk, i, tt):
                for p in range(2):
                    if tt in XW_AT[p]:
                        q = XW_AT[p].index(tt)
                        if tt == min(XW_AT[0] + XW_AT[1]):
                            pe.wait_ge(s_x[1 - i], 16 * ((blk + 1) // 2 + 1) if isinstance(blk, int) else
                                       (blk - i) * 8 + 16 * (1 + i))
                        mm = xw_mm(1 - i, p, q)
                        if tt == max(XW_AT[0] + XW_AT[1]):
                            mm.then_inc(s_xw, 1)

            def route(i, gi, tt):
                if tt == 0:
                    n = 0
                    for k in range(2):
                        for hp, gp in ((hi, gate_hi), (hi, gate_lo), (lo, gate_hi)):
                            mm = pe.matmul(p_lg, hp[:, i, k, :], gp[:, k, :], start=(n == 0), stop=(n == 5))
                            n += 1
                    mm.then_inc(s_lg, 1)
                if tt in ROWS_TURN_AT:
                    pe.wait_ge(s_rt, gi * RT + 1)
                    src = hi if tt == ROWS_TURN_AT[0] else lo
                    for k in range(2):
                        c = (0 if tt == ROWS_TURN_AT[0] else H) + k * P
                        mm = pe.transpose(p_rows[:, c:c + P], src[:, i, k, :], ident16[:])
                    mm.then_inc(s_tr, 1)
                if tt == 14:
                    pe.wait_ge(s_rows, gi * 4 + 4)
                    pe.wait_ge(s_rt, gi * RT + 13)
                    pe.matmul(p_rank, tri[:], chosen[:], start=True, stop=False)
                    pe.matmul(p_rank, all1[:], seen[:, i, :], start=False, stop=True)
                    pe.matmul(p_cnt, all1[:], seen[:, 1 - i, :], start=False, stop=True,
                              skip_group_check=True).then_inc(s_rk, 1)

            def turn_x(q):
                pe.wait_ge(s_xrow, 16 * (q + 1))
                for c in range(2 * KC):
                    mm = pe.transpose(p_x[:, c * P:(c + 1) * P], xrow16[:, c * P:(c + 1) * P], ident16[:])
                mm.then_inc(s_xtp, 1)

            def gate_up(e, up, h, banks, n0, n1):
                prods = [(xpart, w, k) for k in range(KC) for xpart, w in ((k, w_hi), (KC + k, w_hi), (k, w_lo))]
                dst = banks["u" if up else "g"][h]
                for n in range(n0, n1):
                    xpart, w, k = prods[n]
                    a = k * 2 * INNER + up * INNER + h * HALF
                    rhs = w[:, bass.ds(e, 1), a:a + HALF].rearrange("p a c -> p (a c)")
                    mm = pe.matmul(dst[:], x_T[:, xpart, :], rhs, start=(n == 0), stop=(n == 3 * KC - 1),
                                   skip_group_check=True)
                if n1 == 3 * KC:
                    mm.then_inc(s_u if up else s_g, 1)

            def turn_hidden(q, j, banks):
                pe.wait_ge(s_hid, 4 * q + j + 2)
                h, half = j // 2, banks["h"][j // 2]
                if j % 2 == 0:
                    pe.wait_ge(s_hlo, 4 * q + 2 * h + (4 if banks is BETWEEN else 2))
                for n in range(HC // 2):
                    a = (j % 2) * QC + n * P
                    mm = pe.transpose(half[:, a:a + P], hid[:, j * QC + n * P:j * QC + (n + 1) * P], ident32[:])
                if j % 2:
                    mm.then_inc(s_th, 1)

            def down(e, q, c):
                if c % HC == 0:
                    pe.wait_ge(s_hlo, 4 * q + 6 + 2 * (c // HC))
                for n, (hp, w) in enumerate(((hT_hi, w_hi), (hT_hi, w_lo), (hT_lo, w_hi))):
                    rhs = w[:, bass.ds(e, 1), GU + c * H:GU + (c + 1) * H].rearrange("p a c -> p (a c)")
                    mm = pe.matmul(p_y[:, 0:H], hp[:, c * P:(c + 1) * P], rhs, start=(c == 0 and n == 0),
                                   stop=(c == IC - 1 and n == 2))
                if c == IC - 1:
                    mm.then_inc(s_d, 1)

            def keep_warm(n):
                while n > 0:
                    pe.matmul(bank[3][:, 0:min(n, 4) * P], wh_hi[:, 0, 0:P], wh_hi_cols[:, 0:min(n, 4) * P],
                              start=True, stop=True, skip_group_check=True)
                    n -= 4

            experts = {}

            def tile(blk, a, tt):
                q = 2 * (blk - FIRST) + a
                for up in range(2):
                    for h in range(2):
                        at = (G_AT, U_AT)[up][h]
                        if tt == at:
                            if h == 0 and not up:
                                pe.wait_ge(s_xt, 2 * q + 2)
                            pe.wait_ge(s_hid if up else s_sil, 4 * q + 2 * h + 1)
                        if at <= tt < at + 3:
                            gate_up(experts[a], up, h, BETWEEN, 2 * (tt - at), 2 * (tt - at) + 2)
                if tt in TURN_AT:
                    turn_hidden(q, TURN_AT.index(tt), BETWEEN)
                    if tt == TURN_AT[1]:
                        pe.wait_ge(s_sil, 4 * q + 5)
                if tt in DOWN_AT:
                    down(experts[a], q, DOWN_AT.index(tt))

            def step(blk, i, tt, routes, tiles, ahead, last):
                t = i * STEPS + tt
                n = blk * STEPS + tt
                pi, pt = (i, tt - 1) if tt else (1 - i, STEPS - 1)
                if tt in (2, 3):
                    pe.wait_ge(s_clr, 2 * blk + tt - 1)
                pe.wait_ge(s_hi, n + 1)
                for w in (wh_hi, wh_lo):
                    for m in range(2):
                        for k in range(2):
                            pe.matmul(preact(i, tt)[:, B * m:B * m + B], w[:, k, m * P:(m + 1) * P],
                                      hi[:, pi, k, B * pt:B * pt + B], start=False, stop=False, skip_group_check=True)
                pe.wait_ge(s_lo, n + 1)
                for m in range(2):
                    for k in range(2):
                        mm = pe.matmul(preact(i, tt)[:, B * m:B * m + B], wh_hi[:, k, m * P:(m + 1) * P],
                                       lo[:, pi, k, B * pt:B * pt + B], start=False, stop=False, skip_group_check=True)
                mm.then_inc(s_pre, 1)
                xw_too = not last and tt in XW_AT[0] + XW_AT[1]
                if not tiles:
                    keep_warm(6)
                elif not any(at <= tt < at + 12 or tt - at in TURN_AT + DOWN_AT for at in TILE_AT):
                    keep_warm({0: 5, ENTRY_AT[0]: 11, ENTRY_AT[1]: 9, ROWS_TURN_AT[0]: 6, ROWS_TURN_AT[1]: 6, TURN_X_AT[0]: 4, TURN_X_AT[1]: 3}.get(tt, 6 if xw_too else 8))
                elif any(tt - at in TURN_AT for at in TILE_AT) and not xw_too:
                    keep_warm(2)
                for a in range(2):
                    if tiles and tt == ENTRY_AT[a]:
                        experts[a] = entry(pe, 0, 2 * (blk - FIRST) + a)
                if not last:
                    next_xw(blk, i, tt)
                if routes:
                    if tt == 0 and tiles:
                        pe.wait_ge(s_xt, 4 * (blk - FIRST) + 2)
                    route(1 - i, blk - 1, tt)
                if tiles:
                    tile(blk, 0, tt - TILE_AT[0])
                    tile(blk, 1, tt - TILE_AT[1])
                    if tt == TURN_X_AT[1]:
                        pe.wait_ge(s_up, UP * (blk - UP_FROM) + 1)
                        turn_x(2 * (blk - FIRST) + 1)
                if ahead and tt == TURN_X_AT[0]:
                    if not tiles:
                        pe.wait_ge(s_up, UP * (blk - UP_FROM) + 1)
                    turn_x(2 * (blk + 1 - FIRST))

            def pair(pr):
                for i in range(2):
                    for tt in range(STEPS):
                        step(pr * 2 + i, i, tt, **modes(pr, i))

            pe.wait_ge(s_c, 3)
            for _ in range(56):
                pe.matmul(bank[3][:, 0:P], all1[:], all1[:], start=True, stop=True, skip_group_check=True)
            pe.wait_ge(s_prep, 2)
            pe.wait_ge(s_x[0], 16)
            for p in range(2):
                for q in range(6):
                    mm = xw_mm(0, p, q, start=(q == 0))
            mm.then_inc(s_xw, 1)
            pe.wait_ge(s_prep, 6)
            pe.wait_ge(s_cp, 5)
            pair(0)
            pair(1)
            with pe.Fori(FIRST // 2, PAIRS - 1) as pr:
                pair(pr)
            pair(PAIRS - 1)

            def all_gate_up(q, halves=(0, 1)):
                if 0 in halves:
                    experts[0] = entry(pe, 0, q)
                    pe.wait_ge(s_xt, 2 * q + 2)
                    pe.wait_ge(s_hid, 4 * q + 1)
                for h in halves:
                    for up in range(2):
                        gate_up(experts[0], up, h, AFTER, 0, 3 * KC)

            def all_turn(q):
                for j in range(4):
                    turn_hidden(q, j, AFTER)

            def all_down(q, turn=None):
                e = entry(pe, 0, q)
                for c in range(IC):
                    if c == HC and turn is not None:
                        turn_x(turn)
                    down(e, q, c)

            pe.wait_ge(s_hi, T + 1)
            pe.wait_ge(s_lo, T + 1)
            pe.wait_ge(s_xt, 2 * FQ + 2)
            route(1, NBLK - 1, 0)
            all_gate_up(FQ, (0,))
            for tt in ROWS_TURN_AT:
                route(1, NBLK - 1, tt)
            gate_up(experts[0], 0, 1, AFTER, 0, 3 * KC)
            route(1, NBLK - 1, 14)
            gate_up(experts[0], 1, 1, AFTER, 0, 3 * KC)
            pe.wait_ge(s_up, UP * (NBLK - UP_FROM) + 1)
            turn_x(FQ + 1)
            all_turn(FQ)
            all_gate_up(FQ + 1)
            all_down(FQ)
            all_turn(FQ + 1)
            m = tiles_last(pe)
            turn_x(FQ + 2)
            with pe.Fori(FQ + 2, m + LEAST - 1) as q:
                all_gate_up(q)
                all_down(q - 1, q + 1)
                all_turn(q)
            all_gate_up(m + LEAST - 1)
            all_down(m + LEAST - 2)
            all_turn(m + LEAST - 1)
            all_down(m + LEAST - 1)

        @block.scalar
        def _(act):
            def route(gi, tt):
                if tt in ROWS_AT:
                    n = ROWS_AT.index(tt)
                    act.wait_ge(s_tr, gi * 2 + 2)
                    if n == 0 and not is0(gi):
                        act.wait_ge(s_sc, gi * 32)
                    cols = slice((n % 2) * H, (n % 2 + 1) * H)
                    act.copy(rows16[:, n // 2, cols], p_rows[:, cols]).then_inc(s_rows, 1)
                if tt == 12:
                    act.wait_ge(s_rt, gi * RT + 10)
                    act.activation(st[:, 6:7], st[:, 5:6], ACT.Tanh, scale=0.5 / SCALE).then_inc(s_tanh, 1)

            def x_out(q, parts=(0, 1)):
                for n in parts:
                    act.wait_ge(s_xtp, q + 1)
                    act.copy(x_T[:, KC * n:KC * (n + 1), :].rearrange("p c t -> p (c t)"),
                             p_x[:, KC * n * P:KC * (n + 1) * P]).then_inc(s_xt, 1)

            def silu(q, j, banks):
                if j % 2 == 0:
                    act.wait_ge(s_g, 2 * q + 1 + j // 2)
                act.activation(hid[:, j * QC:(j + 1) * QC], banks["g"][j // 2][:, (j % 2) * QC:(j % 2 + 1) * QC],
                               ACT.Silu, scale=1 / SCALE).then_inc(s_sil, 1)

            def hidden_hi(q, j, banks):
                act.wait_ge(s_th, 2 * q + 1 + j // 2)
                act.copy(hT_hi[:, j * QC:(j + 1) * QC],
                         banks["h"][j // 2][:, (j % 2) * QC:(j % 2 + 1) * QC]).then_inc(s_hhi, 1)

            def weigh(q):
                act.wait_ge(s_d, q + 1)
                act.wait_ge(s_mt, 3 * q + 3)
                act.activation(y_sb[:], p_y[:, 0:H], ACT.Copy, scale=weight_now[:, 0:1]).then_inc(s_y, 1)

            def tile(blk, a, tt):
                q = 2 * (blk - FIRST) + a
                if tt in SILU_AT:
                    silu(q, SILU_AT.index(tt), BETWEEN)
                if tt in HI_AT:
                    hidden_hi(q, HI_AT.index(tt), BETWEEN)
                if tt == Y_AT:
                    weigh(q)

            def split(n):
                c, cols = n // 2, slice(n * CHUNK // 2, (n + 1) * CHUNK // 2)
                act.wait_ge(s_st[c % RING], 16 * (c // RING + 1))
                act.activation(w_hi_cols[:, cols], half_stage(n), ACT.Copy, scale=SCALE).then_inc(s_ch, 1)

            def step(blk, i, tt, routes, tiles, ahead, last):
                n = blk * STEPS + tt
                act.wait_ge(s_pre, n + 1)
                src = preact(i, tt).rearrange("p (c b) -> p c b", c=2)
                act.activation(hi[:, i, :, B * tt:B * tt + B], src, ACT.Tanh, scale=1 / SCALE).then_inc(s_hi, 1)
                act.activation(h32[:, 4 * (tt % 2):4 * (tt % 2) + 4], preact(i, tt), ACT.Tanh,
                               scale=1 / SCALE).then_inc(s_h32, 1)
                if routes:
                    route(blk - 1, tt)
                if tiles:
                    tile(blk, 0, tt - TILE_AT[0])
                    tile(blk, 1, tt - TILE_AT[1])
                    if tt in X_OUT_AT[1]:
                        x_out(2 * (blk - FIRST) + 1, (X_OUT_AT[1].index(tt),))
                if ahead and tt in X_OUT_AT[0]:
                    x_out(2 * (blk + 1 - FIRST), (X_OUT_AT[0].index(tt),))
                if split_of(blk, tt) is not None:
                    split(split_of(blk, tt))

            def pair(pr):
                for i in range(2):
                    for tt in range(STEPS):
                        step(pr * 2 + i, i, tt, **modes(pr, i))

            act.wait_ge(s_w, 96)
            act.activation(st[:, 7:8], h0[:, 0, 0:1], ACT.Silu).then_inc(s_sil, 1)
            act.copy(hi[:, 1, :, P - B:P], h0[:]).then_inc(s_hi, 1)
            pair(0)
            pair(1)
            with act.Fori(FIRST // 2, PAIRS - 1) as pr:
                pair(pr)
            pair(PAIRS - 1)

            def all_silu(q):
                for j in range(4):
                    silu(q, j, AFTER)

            def all_hi(q):
                for j in range(4):
                    hidden_hi(q, j, AFTER)

            for tt in ROWS_AT:
                route(NBLK - 1, tt)
            route(NBLK - 1, 12)
            all_silu(FQ)
            x_out(FQ + 1)
            all_hi(FQ)
            all_silu(FQ + 1)
            weigh(FQ)
            m = tiles_last(act)
            x_out(FQ + 2)
            all_hi(FQ + 1)
            with act.Fori(FQ + 2, m + LEAST - 1) as q:
                all_silu(q)
                x_out(q + 1)
                weigh(q - 1)
                all_hi(q)
            all_silu(m + LEAST - 1)
            weigh(m + LEAST - 2)
            all_hi(m + LEAST - 1)
            weigh(m + LEAST - 1)

        @block.vector
        def _(v):
            def route(i, gi, tt):
                def done(k):
                    v.wait_ge(s_rt, gi * RT + k)

                def op(o):
                    o.then_inc(s_rt, 1)

                if tt == 1:
                    v.wait_ge(s_lg, gi + 1)
                    op(v.tensor_copy(lg[:], p_lg))
                if tt == 3:
                    done(1)
                    op(v.tensor_reduce(st[:, 0:1], lg[:], AX.X, ALU.max))
                if tt == 4:
                    done(2)
                    op(v.scalar_tensor_tensor(out=pick[:], in0=lg[:], scalar=st[:, 0:1], in1=rev[:],
                                              op0=ALU.is_equal, op1=ALU.mult))
                if tt == 5:
                    done(3)
                    op(v.tensor_reduce(st[:, 4:5], pick[:], AX.X, ALU.max))
                if tt == 6:
                    done(4)
                    op(v.tensor_scalar(oh1[:], rev[:], st[:, 4:5], None, ALU.is_equal))
                if tt == 7:
                    done(5)
                    op(v.scalar_tensor_tensor(out=lg2[:], in0=oh1[:], scalar=NEG, in1=lg[:],
                                              op0=ALU.mult, op1=ALU.add))
                if tt == 8:
                    done(6)
                    op(v.tensor_reduce(st[:, 1:2], lg2[:], AX.X, ALU.max))
                if tt == 9:
                    done(7)
                    op(v.scalar_tensor_tensor(out=pick[:], in0=lg2[:], scalar=st[:, 1:2], in1=rev[:],
                                              op0=ALU.is_equal, op1=ALU.mult))
                if tt == 10:
                    done(8)
                    op(v.tensor_reduce(st[:, 4:5], pick[:], AX.X, ALU.max))
                    op(v.tensor_tensor(st[:, 5:6], st[:, 0:1], st[:, 1:2], ALU.subtract))
                if tt == 11:
                    done(10)
                    op(v.tensor_scalar(oh2[:], rev[:], st[:, 4:5], None, ALU.is_equal))
                if tt == 12:
                    done(11)
                    op(v.tensor_tensor(chosen[:], oh1[:], oh2[:], ALU.add))
                if tt == 13:
                    done(12)
                    op(v.tensor_tensor(seen[:, 1 - i, :], seen[:, i, :], chosen[:], ALU.add))
                if tt == 15:
                    v.wait_ge(s_rk, gi + 1)
                    done(13)
                    op(v.tensor_tensor(rank[:], p_rank, base[:], ALU.add))
                if tt == 16:
                    done(14)
                    op(v.tensor_tensor_reduce(pick[:], oh1[:], rank[:], 1.0, 0.0, ALU.mult, ALU.add, st[:, 2:3]))
                if tt == 17:
                    done(15)
                    op(v.tensor_tensor_reduce(pick[:], oh2[:], rank[:], 1.0, 0.0, ALU.mult, ALU.add, st[:, 3:4]))
                    v.wait_ge(s_tanh, gi + 1)
                    if not is0(gi):
                        v.wait_ge(s_sc, gi * 32)
                    op(v.tensor_scalar(meta[:, 0, 1:2], st[:, 6:7], 0.5 / SCALE, 0.5 / SCALE, ALU.mult, ALU.add))
                if tt == 18:
                    op(v.tensor_scalar(meta[:, 1, 1:2], st[:, 6:7], -0.5 / SCALE, 0.5 / SCALE, ALU.mult, ALU.add))
                    op(v.tensor_copy(meta[:, :, 0:1], tok[:].unsqueeze(1).to_broadcast([P, 2, 1])))
                if tt == 19:
                    done(19)
                    op(v.tensor_scalar(tok[:], tok[:], float(STEPS), None, ALU.add))
                    v.wait_ge(s_rows, gi * 4 + 4)
                    op(v.tensor_copy(slot[:], st[:, 2:4]))

            def update(n, k, flush=False):
                if k == 15:
                    regs["at"] = nc.s_assert_within(v.value_load(qi), 0, QMAX, skip_runtime_bounds_check_because=(
                        "all rows fill QMAX tiles at most, with those of the slots passed over"))
                if k:
                    v.wait_ge(s_up, UP * n + k)
                j3 = cmp[:, 0:WINDOW * E].rearrange("p (j e) -> p j e", e=E)
                q3 = cmp[:, 0:E * NBLK].rearrange("p (e q) -> p e q", e=E)
                e3 = cmp[:, 0:E * E].rearrange("p (e q) -> p e q", e=E)

                def each(a):
                    return a.unsqueeze(1).to_broadcast([1, WINDOW, E])

                if k == 0:
                    o = v.tensor_copy(cnt, p_cnt[0:1, :])
                elif k == 1:
                    o = v.tensor_tensor(q3, cnt.unsqueeze(2).to_broadcast([1, E, NBLK]),
                                        (frow if flush else qrow).unsqueeze(1).to_broadcast([1, E, NBLK]), ALU.is_ge)
                elif k == 2:
                    o = v.tensor_reduce(full, q3, AX.X, ALU.add)
                elif k == 3:
                    o = v.tensor_tensor(new, full, had[:, 0:E], ALU.subtract)
                elif k == 4:
                    o = v.tensor_tensor(e3, tri8, new.unsqueeze(1).to_broadcast([1, E, E]), ALU.mult)
                elif k == 5:
                    o = v.tensor_reduce(upto, e3, AX.X, ALU.add)
                elif k == 6:
                    o = v.tensor_tensor(j3, irow.unsqueeze(2).to_broadcast([1, WINDOW, E]), each(upto), ALU.is_ge)
                elif k == 7:
                    o = v.tensor_reduce(ej, j3, AX.X, ALU.add)
                elif k == 8:
                    o = v.tensor_tensor(step_e, had[:, 1:E + 1], had[:, 0:E], ALU.subtract)
                elif k == 9:
                    o = v.tensor_tensor(step_e, step_e, new, ALU.subtract)
                elif k == 10:
                    o = v.tensor_tensor(j3, j3, each(step_e), ALU.mult)
                elif k == 11:
                    o = v.tensor_reduce(sj, j3, AX.X, ALU.add)
                elif k == 12:
                    o = v.tensor_tensor(sj, sj, irow, ALU.add)
                elif k == 13:
                    o = v.tensor_scalar(sj, sj, had[:, 0:1], float(P), ALU.add, ALU.mult)
                elif k == 14:
                    o = v.scalar_tensor_tensor(out=gj, in0=ej, scalar=float(REGION), in1=sj,
                                               op0=ALU.mult, op1=ALU.add)
                elif k == 15:
                    o = v.tensor_scalar(queue[0:1, 0, bass.ds(regs["at"], WINDOW)], ej, float(E - 1), None, ALU.min)
                elif k == 16:
                    o = v.tensor_copy(queue[0:1, 1, bass.ds(regs["at"], WINDOW)], gj)
                elif k == 17:
                    o = v.tensor_copy(had[:, 0:E], full)
                elif k == 18:
                    o = v.tensor_scalar(floor, floor, 2.0, None, ALU.add)
                elif k == 19:
                    o = v.scalar_tensor_tensor(out=place, in0=upto[:, E - 1:E], scalar=place, in1=floor,
                                               op0=ALU.add, op1=ALU.max)
                elif k == 20:
                    o = v.tensor_copy(qi, place)
                else:
                    o = v.tensor_scalar(left, place, -float(LEAST), 0.0, ALU.add, ALU.max)
                o.then_inc(s_up, 1)

            regs = {}

            def times_up(q, j, banks):
                v.wait_ge(s_sil, 4 * q + 2 + j)
                v.wait_ge(s_u, 2 * q + 1 + j // 2)
                part = hid[:, j * QC:(j + 1) * QC]
                v.scalar_tensor_tensor(out=part, in0=banks["u"][j // 2][:, (j % 2) * QC:(j % 2 + 1) * QC],
                                       scalar=1 / SCALE, in1=part, op0=ALU.mult, op1=ALU.mult).then_inc(s_hid, 1)

            def hidden_lo(q, j, banks):
                v.wait_ge(s_hhi, 4 * q + 2 * (j // 2) + 2)
                cols = slice(j * QC, (j + 1) * QC)
                v.tensor_tensor(hT_lo[:, cols], banks["h"][j // 2][:, (j % 2) * QC:(j % 2 + 1) * QC],
                                hT_hi[:, cols], ALU.subtract).then_inc(s_hlo, 1)

            def take(q):
                v.wait_ge(s_xrow, 16 * (q + 1))
                if not is0(q):
                    v.wait_ge(s_mt, 3 * q)
                v.tensor_copy(meta_in[:], xrow_meta).then_inc(s_mt, 1)

            def shift(q):
                v.wait_ge(s_mt, 3 * q + 1)
                if not is0(q):
                    v.wait_ge(s_scat, 16 * q)
                v.tensor_copy(place_now[:], meta_in[:, 0:1]).then_inc(s_mt, 1)
                v.tensor_copy(weight_now[:], meta_in[:, 1:2]).then_inc(s_mt, 1)

            def tile(blk, a, tt):
                q = 2 * (blk - FIRST) + a
                if tt in MUL_AT:
                    times_up(q, MUL_AT.index(tt), BETWEEN)
                if tt in LO_AT:
                    hidden_lo(q, LO_AT.index(tt), BETWEEN)
                if tt == SHIFT_AT:
                    shift(q)

            def split(n):
                v.wait_ge(s_ch, n + 1)
                cols = slice(n * CHUNK // 2, (n + 1) * CHUNK // 2)
                v.scalar_tensor_tensor(out=w_lo_cols[:, cols], in0=half_stage(n), scalar=SCALE,
                                       in1=w_hi_cols[:, cols], op0=ALU.mult, op1=ALU.subtract).then_inc(s_cl, 1)

            def step(blk, i, tt, routes, tiles, ahead, last):
                n = blk * STEPS + tt
                v.wait_ge(s_h32, n + 1)
                v.tensor_tensor(lo[:, i, :, B * tt:B * tt + B],
                                h32[:, 4 * (tt % 2):4 * (tt % 2) + 4].rearrange("p (c b) -> p c b", c=2),
                                hi[:, i, :, B * tt:B * tt + B], ALU.subtract).then_inc(s_lo, 1)
                if tt < 2:
                    v.memset(xw[tt % 2][:, (1 - i) * P:(2 - i) * P], 0.0).then_inc(s_clr, 1)
                if routes:
                    route(1 - i, blk - 1, tt)
                    if not isinstance(blk, int) or blk >= UP_FROM:
                        if tt == 16:
                            update(blk - UP_FROM, 0)
                        if last and tt == 17:
                            v.wait_ge(s_up, UP * (blk - UP_FROM) + 1)
                            v.tensor_copy(counts_i[:], cnt).then_inc(s_cnt, 1)
                        if tt in UPDATE_AT[1:]:
                            update(blk - UP_FROM, UPDATE_AT.index(tt))
                if tiles:
                    tile(blk, 0, tt - TILE_AT[0])
                    tile(blk, 1, tt - TILE_AT[1])
                    if tt == TAKE_AT[1]:
                        take(2 * (blk - FIRST) + 1)
                if ahead and tt == TAKE_AT[0]:
                    take(2 * (blk + 1 - FIRST))
                if split_of(blk, tt) is not None:
                    split(split_of(blk, tt))

            def pair(pr):
                for i in range(2):
                    for tt in range(STEPS):
                        step(pr * 2 + i, i, tt, **modes(pr, i))

            v.memset(ones[:], 1.0).then_inc(s_c, 1)
            v.memset(all1[:], 1.0).then_inc(s_c, 1)
            v.memset(seen[:], 0.0).then_inc(s_c, 1)
            v.memset(rows[:, :, H:], 0.0)
            v.memset(had, 0.0)
            v.memset(place, 0.0)
            v.memset(qi.bitcast(F32), 0.0).then_inc(s_hlo, 4)
            v.memset(floor, -2.0).then_inc(s_hid, 1)
            v.wait_ge(s_w, 96)
            v.tensor_scalar(wx_sb[:], wx_sb[:], SCALE, None, ALU.mult).then_inc(s_prep, 1)
            v.tensor_scalar(b_sb[:], b_sb[:], SCALE, None, ALU.mult).then_inc(s_prep, 1)
            v.tensor_scalar(wh_hi[:], wh_sb, SCALE, None, ALU.mult).then_inc(s_prep, 1)
            v.tensor_scalar(gate_hi[:], gate_sb, SCALE, None, ALU.mult).then_inc(s_prep, 1)
            v.wait_ge(s_prep, 4)
            v.scalar_tensor_tensor(out=wh_lo[:], in0=wh_sb, scalar=SCALE, in1=wh_hi[:],
                                   op0=ALU.mult, op1=ALU.subtract).then_inc(s_prep, 1)
            v.scalar_tensor_tensor(out=gate_lo[:], in0=gate_sb, scalar=SCALE, in1=gate_hi[:],
                                   op0=ALU.mult, op1=ALU.subtract).then_inc(s_prep, 1)
            v.wait_ge(s_hi, 1)
            v.tensor_tensor(lo[:, 1, :, P - B:P], h0[:], hi[:, 1, :, P - B:P], ALU.subtract).then_inc(s_lo, 1)
            v.wait_ge(s_cp, 5)
            v.wait_ge(s_padc, 3)
            v.wait_ge(s_hid, 1)
            pair(0)
            pair(1)
            with v.Fori(FIRST // 2, PAIRS - 1) as pr:
                pair(pr)
            pair(PAIRS - 1)

            def all_times_up(q):
                for j in range(4):
                    times_up(q, j, AFTER)

            def all_lo(q):
                for j in range(4):
                    hidden_lo(q, j, AFTER)

            for tt in range(1, 14):
                route(1, NBLK - 1, tt)
            for tt in range(15, 20):
                route(1, NBLK - 1, tt)
            last = NBLK - UP_FROM
            update(last, 0)
            all_times_up(FQ)
            all_lo(FQ)
            shift(FQ)
            take(FQ + 1)
            for k in range(1, UP):
                update(last, k, flush=True)
            all_times_up(FQ + 1)
            m = tiles_last(v)
            all_lo(FQ + 1)
            shift(FQ + 1)
            take(FQ + 2)
            with v.Fori(FQ + 2, m + LEAST - 1) as q:
                all_times_up(q)
                all_lo(q)
                shift(q)
                take(q + 1)
            all_times_up(m + LEAST - 1)
            all_lo(m + LEAST - 1)
            shift(m + LEAST - 1)

        @block.gpsimd
        def _(pool):
            def iota(out, pattern, base_, mult=0):
                return pool.iota(out, pattern, base=base_, channel_multiplier=mult,
                                 allow_small_or_imprecise_dtypes=True)

            pool.memset(ident32[:], 0.0).then_inc(s_cp, 1)
            pool.memset(tri[:], 1.0).then_inc(s_cp, 1)
            pool.memset(tri8, 1.0).then_inc(s_padc, 1)
            pool.memset(pad[:], 0.0).then_inc(s_padc, 1)
            pool.wait_ge(s_cp, 2)
            pool.affine_select(out=ident32[:], in_=ident32[:], compare_op=ALU.not_equal, fill=1.0, base=0,
                               pattern=[[-1, P]], channel_multiplier=1).then_inc(s_cp, 1)
            pool.affine_select(out=tri[:], in_=tri[:], compare_op=ALU.is_gt, fill=0.0, base=0,
                               pattern=[[1, P]], channel_multiplier=-1)
            iota(rev[:], [[-1, E]], E)
            iota(base[:], [[REGION, E]], 0).then_inc(s_cp, 1)
            pool.wait_ge(s_cp, 4)
            pool.tensor_copy(ident16[:], ident32[:]).then_inc(s_cp, 1)
            pool.wait_ge(s_padc, 2)
            pool.affine_select(out=tri8, in_=tri8, compare_op=ALU.is_ge, fill=0.0, base=0,
                               pattern=[[1, E], [-1, E]], channel_multiplier=0)
            iota(irow, [[1, WINDOW]], 0)
            iota(qrow, [[P, NBLK]], P)
            iota(frow, [[P, NBLK]], 1)
            iota(pad[:, H:H + 1], [[0, 1]], TOK, 1).then_inc(s_padc, 1)

            routed = pool.alloc_register("routed_count")
            ready = pool.alloc_register("ready_count")
            pool.reg_mov(routed, RT)
            pool.reg_mov(ready, 1)

            def scatter_rows():
                pool.wait_ge(s_cp, 5)
                pool.wait_ge(s_rt, routed)
                for k in range(2):
                    pool.indirect_dma_start(rows_dram, bass.IndirectOffsetOnAxis(ap=slot[:, k:k + 1], axis=0),
                                            rows[:, k, :], None).then_inc(s_sc, 16)
                pool.reg_add(routed, routed, RT)

            def add_results(s=s_scat):
                pool.wait_ge(s_acc, 16 * (2 + WINDOW))
                pool.wait_ge(s_y, ready)
                pool.indirect_dma_start(out, bass.IndirectOffsetOnAxis(ap=place_now[:, 0:1], axis=0),
                                        y_sb[:], None, compute_op=ALU.add).then_inc(s, 16)
                pool.reg_add(ready, ready, 1)

            for _ in range(FIRST - 1):
                scatter_rows()
            with pool.Fori(FIRST, NBLK):
                scatter_rows()
                add_results()
                add_results()
            pool.wait_ge(s_fill, 32 * E)
            scatter_rows()
            add_results()
            add_results()
            m = tiles_last(pool)
            with pool.Fori(FQ + 2, m + LEAST - 1):
                add_results()
            add_results(s_scat_last)


def kernel(x, cond_1024, L0_cond_Wx, L0_cond_Wh, L0_cond_b, L0_ffn_gate_w, L0_ffn_wg, L0_ffn_wu, L0_ffn_wd):
    import concourse.bacc as bacc
    import numpy as np
    from concourse.bass_utils import run_bass_kernel_spmd

    a = np.asarray
    x = a(x)
    b, t, d = x.shape
    e, inner, _ = L0_ffn_wg.shape
    kc = d // P

    def chunks(m):
        return np.ascontiguousarray(m.reshape(kc, P, *m.shape[1:]).swapaxes(0, 1))

    wg = a(L0_ffn_wg).transpose(2, 0, 1).reshape(kc, P, e, 1, inner)
    wu = a(L0_ffn_wu).transpose(2, 0, 1).reshape(kc, P, e, 1, inner)
    gu = np.concatenate([wg, wu], axis=3).transpose(1, 2, 0, 3, 4).reshape(P, e, -1)
    dn = a(L0_ffn_wd).transpose(2, 0, 1).reshape(inner // P, P, e, d).transpose(1, 2, 0, 3).reshape(P, e, -1)
    arrays = {
        "xT": chunks(x.transpose(2, 1, 0).reshape(d, t * b)),
        "x_in": np.ascontiguousarray(x),
        "h0T": chunks(a(cond_1024).T),
        "wx_in": np.ascontiguousarray(a(L0_cond_Wx)),
        "wh_in": np.ascontiguousarray(a(L0_cond_Wh)),
        "bias_in": np.ascontiguousarray(a(L0_cond_b)).reshape(1, -1),
        "gateT": chunks(a(L0_ffn_gate_w).T),
        "w_all": np.ascontiguousarray(np.concatenate([gu, dn], axis=2)),
        "tok0": np.array([[(p % b) * t + p // b] for p in range(P)], np.float32),
    }
    nc = bacc.Bacc("TRN2", target_bir_lowering=False, num_devices=1, dynamic_dma_scratch_size=4096)
    args = [nc.dram_tensor(k, v.shape, mybir.dt.from_np(v.dtype), kind="ExternalInput").ap() for k, v in arrays.items()]
    out = nc.dram_tensor("out", (b * t + P, d), F32, kind="ExternalOutput").ap()
    build(nc, *args, out)
    result = run_bass_kernel_spmd(nc, [arrays], core_ids=[0])
    return result.results[0]["out"][:b * t].reshape(b, t, d)
```
